# Optimizing a Trainium2 kernel written in Bass

```python
import numpy as np
import jax
import jax.numpy as jnp

def _softmax(x, axis=-1):
    return jax.nn.softmax(x, axis=axis)

def _gelu(x):
    return jax.nn.gelu(x, approximate=True)

def _silu(x):
    return jax.nn.silu(x)

def _sigmoid(x):
    return jax.nn.sigmoid(x)

def _layernorm(x, axis=-1, eps=1e-05):
    m = jnp.mean(x, axis=axis, keepdims=True)
    v = jnp.var(x, axis=axis, keepdims=True)
    return (x - m) / jnp.sqrt(v + eps)

def _scatter_add(tgt, idx, src, axis=0):
    return tgt.at[idx].add(src)

def _segment_sum(src, seg, n):
    return jax.ops.segment_sum(src, seg, n)
kernel_name = 'mk_xattn_ffn_d1_seqx_r4_165469'

def setup_inputs(seed: int=0):
    np.random.seed(seed)
    _w = jnp.asarray

    def _rec_inputs():
        import jax
        import jax.numpy as jnp
        _rk = jax.random.key(seed)
        x = -0.0005207 + 1.001 * jax.random.normal(jax.random.fold_in(_rk, 1), (8, 112, 512), jnp.float32)
        _lenS = 112 - jax.random.randint(jax.random.fold_in(_rk, 7), (8,), 0, max(1, 112 // 4) + 1, jnp.int32)
        _lenS2 = 375 - jax.random.randint(jax.random.fold_in(_rk, 8), (8,), 0, max(1, 375 // 4) + 1, jnp.int32)
        _ctx_2048P = jax.random.normal(jax.random.fold_in(_rk, 12), (8, 16, 512), jnp.float32)
        _ctx_2048c = jax.random.dirichlet(jax.random.fold_in(_rk, 512), 0.3 * jnp.ones((16,), jnp.float32), (8, 375))
        _ctx_2048t = jnp.einsum('bsk,bkd->bsd', _ctx_2048c, _ctx_2048P)
        _ctx_2048t = _ctx_2048t * jax.lax.rsqrt(jnp.mean(jnp.square(_ctx_2048t)) + 1e-12) * 0.953939
        ctx_2048 = -5.72187e-05 + 0.999849 * (_ctx_2048t + 0.3 * jax.random.normal(jax.random.fold_in(_rk, 612), (8, 375, 512), jnp.float32))
        _validS = jnp.arange(112)[None, :] < _lenS[:, None]
        _validS2 = jnp.arange(375)[None, :] < _lenS2[:, None]
        _causal = jnp.tril(jnp.ones((112, 112), dtype=bool))
        mask_BxSx4224_bf0 = jnp.logical_not(jnp.ones((8, 112, 1056), dtype=bool))
        return (x, ctx_2048, mask_BxSx4224_bf0)
    x, ctx_2048, mask_BxSx4224_bf0 = _rec_inputs()

    def _L0_xattn_setup():
        import jax, jax.numpy as jnp
        import numpy as np
        import math
        DIM = 512
        B, Q_LEN, KV_LEN = (8, 128, 1024)
        key = jax.random.key(seed)
        ks = jax.random.split(key, 8)
        x = jax.random.normal(ks[0], (B, Q_LEN, DIM), dtype=jnp.float32)
        mask = jnp.zeros((B, Q_LEN, KV_LEN + Q_LEN), dtype=bool)
        k_cache = jax.random.normal(ks[1], (B, KV_LEN, DIM), dtype=jnp.float32)
        v_cache = jax.random.normal(ks[2], (B, KV_LEN, DIM), dtype=jnp.float32)
        scale = 1.0 / math.sqrt(DIM)
        wq = jax.random.normal(ks[3], (DIM, DIM), dtype=jnp.float32) * scale
        wk = jax.random.normal(ks[4], (DIM, DIM), dtype=jnp.float32) * scale
        wv = jax.random.normal(ks[5], (DIM, DIM), dtype=jnp.float32) * scale
        wo = jax.random.normal(ks[6], (DIM, DIM), dtype=jnp.float32) * scale
        return {'x': x, 'mask': mask, 'k_cache': k_cache, 'v_cache': v_cache, 'wq': wq, 'wk': wk, 'wv': wv, 'wo': wo}
    _L0_xattn_all = _L0_xattn_setup()
    _L0_xattn_in = {k: v for k, v in _L0_xattn_all.items() if k in ('wq', 'wk', 'wv', 'wo')}
    del _L0_xattn_all

    def _L0_ffn_setup():
        import jax, jax.numpy as jnp
        import numpy as np
        B, S, H, I, E, K = (4, 512, 512, 1024, 8, 2)
        key = jax.random.key(seed)
        k1, k2, k3, k4 = jax.random.split(key, 4)
        return {'hidden_states': jax.random.normal(k1, (B, S, H), dtype=jnp.float32), 'gate_weight': jax.random.normal(k2, (E, H), dtype=jnp.float32) * 0.02, 'gate_up_proj': jax.random.normal(k3, (E, 2 * I, H), dtype=jnp.float32) * 0.02, 'down_proj': jax.random.normal(k4, (E, H, I), dtype=jnp.float32) * 0.02}
    _L0_ffn_all = _L0_ffn_setup()
    _L0_ffn_in = {k: v for k, v in _L0_ffn_all.items() if k in ('gate_weight', 'gate_up_proj', 'down_proj')}
    del _L0_ffn_all
    return {'x': x, 'ctx_2048': ctx_2048, 'mask_BxSx4224_bf0': mask_BxSx4224_bf0, 'L0_xattn_wq': _L0_xattn_in['wq'], 'L0_xattn_wk': _L0_xattn_in['wk'], 'L0_xattn_wv': _L0_xattn_in['wv'], 'L0_xattn_wo': _L0_xattn_in['wo'], 'L0_ffn_gate_weight': _L0_ffn_in['gate_weight'], 'L0_ffn_gate_up_proj': _L0_ffn_in['gate_up_proj'], 'L0_ffn_down_proj': _L0_ffn_in['down_proj']}

def reference(x, ctx_2048, mask_BxSx4224_bf0, L0_xattn_wq, L0_xattn_wk, L0_xattn_wv, L0_xattn_wo, L0_ffn_gate_weight, L0_ffn_gate_up_proj, L0_ffn_down_proj):
    import jax
    import jax.numpy as jnp

    def _L0_xattn_ref(x, mask, k_cache, v_cache, wq, wk, wv, wo):
        import jax, jax.numpy as jnp
        import numpy as np
        import math
        DIM = 512
        B, Q_LEN, KV_LEN = (8, 128, 1024)
        q = jnp.einsum('bsd,ed->bse', x, wq)
        k_new = jnp.einsum('bsd,ed->bse', x, wk)
        v_new = jnp.einsum('bsd,ed->bse', x, wv)
        k = jnp.concatenate([k_cache, k_new], axis=1)
        v = jnp.concatenate([v_cache, v_new], axis=1)
        scale = 1.0 / math.sqrt(q.shape[-1])
        scores = jnp.einsum('bqd,bkd->bqk', q, k) * scale
        attn = jax.nn.softmax(scores, axis=-1)
        out = jnp.einsum('bqk,bkd->bqd', attn, v)
        return jnp.einsum('bqd,ed->bqe', out, wo)

    def _L0_ffn_ref(hidden_states, gate_weight, gate_up_proj, down_proj):
        import jax, jax.numpy as jnp
        import numpy as np
        B, S, H, I, E, K = (4, 512, 512, 1024, 8, 2)
        b, s, h = hidden_states.shape
        num_experts, top_k = (gate_weight.shape[0], K)
        x = hidden_states.reshape(-1, h)
        router_logits = x @ gate_weight.T
        probs = jax.nn.softmax(router_logits.astype(jnp.float32), axis=-1)
        top_v, top_i = jax.lax.top_k(probs, top_k)
        top_v = top_v / top_v.sum(axis=-1, keepdims=True)
        combine_w = jnp.einsum('tke,tk->te', jax.nn.one_hot(top_i, num_experts, dtype=top_v.dtype), top_v).astype(x.dtype)

        def expert_step(acc, inp):
            gu, dp, w = inp
            gate, up = jnp.split(x @ gu.T, 2, axis=-1)
            hidden = jax.nn.silu(gate) * up
            y = hidden @ dp.T
            return (acc + w[:, None] * y, None)
        out, _ = jax.lax.scan(expert_step, jnp.zeros_like(x), (gate_up_proj, down_proj, combine_w.T))
        return out.reshape(b, s, h)
    x = x + _L0_xattn_ref(_layernorm(x, axis=-1), mask_BxSx4224_bf0, ctx_2048, ctx_2048, L0_xattn_wq, L0_xattn_wk, L0_xattn_wv, L0_xattn_wo)
    x = x + _L0_ffn_ref(_layernorm(x, axis=-1), L0_ffn_gate_weight, L0_ffn_gate_up_proj, L0_ffn_down_proj)
    return x

_drawn_inputs = setup_inputs


def setup_inputs(seed=0):
    import zlib

    import numpy as np

    out = dict(_drawn_inputs(seed))
    spreads = {}
    factors = {}
    for name, (base, spread) in spreads.items():
        noise = np.random.default_rng([zlib.crc32(name.encode()), seed]).standard_normal(out[name].shape)
        drawn = base * np.exp(spread * noise) if base else spread * noise
        out[name] = jnp.asarray(drawn.astype(out[name].dtype))
    for name, factor in factors.items():
        out[name] = (out[name] * factor).astype(out[name].dtype)
    return out
```

```python
import concourse.bass as bass
from concourse import mybir
from contextlib import ExitStack

F32 = mybir.dt.float32
F32R = mybir.dt.float32r
BF16 = mybir.dt.bfloat16
I32 = mybir.dt.int32
U32 = mybir.dt.uint32
ACT = mybir.ActivationFunctionType
ALU = mybir.AluOpType
AX = mybir.AxisListType

NB = 8
S = 112
D = 512
KT = D // 128
C = 375
NEW = 0
CTX = S
KEYS = S + C
KP = KEYS + 1
CROWS = [128, 128, C - 256]
NE = 8
I = 1024
IT = I // 128
CAP = 256
ROUNDS = 4
RW = D + 2
RROWS = NE * CAP
ROWS = ROUNDS * RROWS + 2 * CAP
TOK = NB * S
OUTR = TOK + CAP
SCALE = float(D) ** -0.5
EPS = 1e-5
PAIRS = NB // 2
ZW = 1028


def build_kernel(nc, x, ctxt, wq, wk, wv, wo, gate_w, gate_up, down, out):
    slots = nc.dram_tensor("slots", (ROWS, RW), F32, kind="Internal").ap()

    stack = ExitStack()
    with stack:
        def sem(name):
            return stack.enter_context(nc.semaphore(name))

        def pb(name):
            return stack.enter_context(nc.psum_tensor(name, [128, 512], F32))

        top = [(nc.sbuf_base + 63) // 64 * 64]

        def at(name, shape, dt, offset):
            return nc.alloc_sbuf_tensor_at(name, shape, dt, offset=offset)

        def size(shape, dt):
            n = 1
            for s in shape[1:]:
                n *= s
            return (n * (2 if dt == BF16 else 4) + 31) // 32 * 32

        def sb(name, shape, dt):
            offset = top[0]
            top[0] += size(shape, dt)
            return at(name, shape, dt, offset)

        ident = sb("ident", [128, 128], F32)
        zero = sb("zero", [128, ZW], F32)
        tri = sb("tri", [S, S], BF16)
        ones = sb("ones", [S, S], BF16)
        iota8 = sb("iota8", [S, NE], F32)
        ebase = sb("ebase", [S, NE], F32)
        padid = sb("padid", [128, 2], F32)
        half = sb("half", [128, 8], F32)
        iotai = sb("iotai", [128, 24], I32)
        w_all = sb("w_all", [S, NB, 2], F32)
        row_all = sb("row_all", [S, NB, 2], I32)
        most = sb("most", [S, 2], F32)
        mosti = sb("mosti", [S, 2], I32)
        yidx = sb("yidx", [128, 2, 2], I32)
        spare = sb("spare", [1, 1], F32)
        flags = sb("flags", [1, 64], F32)
        yidt = sb("yidt", [128, 2, 2], F32)
        st = sb("st", [S, 2, 6], F32)
        mv1 = sb("mv1", [S, 2, 2], F32)
        ve1 = sb("ve1", [S, 2, 1], F32)
        rs1 = sb("rs1", [S, 2, 1], F32)
        st2 = sb("st2", [S, 2, 6], F32)
        mv2 = sb("mv2", [S, 2, 2], F32)
        ve2 = sb("ve2", [S, 2, 1], F32)
        rs2 = sb("rs2", [S, 2, 1], F32)
        mx = sb("mx", [S, 2, 1], F32)
        nm = sb("nm", [S, 2, 1], F32)
        esum = sb("esum", [S, 2, 1], F32)
        rinv = sb("rinv", [S, 2, 1], F32)
        lgs = sb("lgs", [S, 2, 8], F32)
        mx8 = sb("mx8", [S, 2, 8], F32)
        ix8 = sb("ix8", [S, 2, 8], U32)
        ixf = sb("ixf", [S, 2, 2], F32)
        mask = sb("mask", [S, 2, 2, 8], F32)
        mboth = sb("mboth", [S, 2, 8], BF16)
        msum = sb("msum", [S, 2, 8], BF16)
        pos = sb("pos", [S, 2, 8], F32)
        rr = sb("rr", [S, 2, 8], F32)
        rr2 = sb("rr2", [S, 2, 8], F32)
        rr3 = sb("rr3", [S, 2, 8], F32)
        rb = sb("rb", [S, 2, 8], F32)
        row8 = sb("row8", [S, 2, 8], F32)
        junk = sb("junk", [S, 2, 2, 8], F32)
        rowf = sb("rowf", [S, 2, 2], F32)
        dl = sb("dl", [S, 2, 1], F32)
        el = sb("el", [S, 2, 1], F32)
        el1 = sb("el1", [S, 2, 1], F32)
        wts = sb("wts", [S, 2, 2], F32)
        idx = [[sb(f"idx{a}{s}", [S, 1], I32) for s in range(2)] for a in range(2)]
        gwT = sb("gwT", [128, KT, NE], F32)
        o_xn2 = top[0]
        xn2_all = sb("xn2_all", [S, NB, D], F32)
        xr = [sb(f"xr{a}", [S, 2, RW], F32) for a in range(2)]

        o_w = top[0]
        wTh = [None] * 4
        wTl = [None] * 4
        for n in range(4):
            wTh[n] = sb(f"wTh{n}", [128, KT, D], F32R)
            wTl[n] = sb(f"wTl{n}", [128, KT, D], F32R)
        wnat = [at(f"wnat{n}", [128, KT, D], F32, o_xn2 + n * KT * D * 4) for n in range(2)]
        x_all = sb("x_all", [S, NB, D], F32)
        o_xt = top[0]
        xTh = sb("xTh", [128, KT, 2 * S], F32R)
        xTl = sb("xTl", [128, KT, 2 * S], F32R)
        qTh = sb("qTh", [128, KT, 2 * S], F32R)
        qTl = sb("qTl", [128, KT, 2 * S], F32R)
        o_keys = top[0]
        kTh = sb("kTh", [128, KT, 2, KP], F32R)
        kTl = sb("kTl", [128, KT, 2, KP], F32R)
        o_cn = top[0]
        cn = [sb(f"cn{a}", [128, 3, D], F32) for a in range(2)]
        vl = [at(f"vl{a}", [128, 3, D], F32R, o_cn + a * 3 * D * 4) for a in range(2)]
        vh = [sb(f"vh{a}", [128, 3, D], F32R) for a in range(2)]
        o_vn = top[0]
        vnh = [sb(f"vnh{a}", [S, D], F32R) for a in range(2)]
        vnl = [sb(f"vnl{a}", [S, D], F32R) for a in range(2)]
        o_e = top[0]
        ex = [sb(f"ex{a}", [S, 512], F32) for a in range(2)]
        aTh = sb("aTh", [128, 4, S], F32R)
        aTl = sb("aTl", [128, 4, S], F32R)
        gwn = at("gwn", [NE, D], F32, top[0])
        on = sb("on", [S, D], F32)
        oTh = sb("oTh", [128, KT, S], F32R)
        oTl = sb("oTl", [128, KT, S], F32R)
        xn = [sb(f"xn{a}", [S, D], F32) for a in range(2)]
        x2T = sb("x2T", [128, KT, S], F32)
        assert top[0] <= nc.sbuf_usable_end, (top[0], nc.sbuf_usable_end)

        NG = 4
        ng = [at(f"ng{n}", [128, 2, D], F32, o_w + n * 4096) for n in range(NG)]
        dn = [at(f"dn{n}", [128, KT, I], F32, o_w + 16384 + n * 16384) for n in range(2)]
        wt = [[at(f"m{w}{h}{n}", [128, 512], F32R, o_keys + ((n * 3 + w) * 2 + h) * 2048)
               for w in range(3) for h in range(2)] for n in range(2)]
        eh = [at(f"eh{n}", [128, KT, CAP], F32R, o_cn + n * 8192) for n in range(2)]
        el_ = [at(f"el_{n}", [128, KT, CAP], F32R, o_cn + n * 8192 + 4096) for n in range(2)]
        xe = [at(f"xe{n}", [128, 2, RW], F32, o_xt + n * 4128) for n in range(2)]
        hs = [at(f"hs{n}", [128, CAP], F32, o_vn + n * 1024) for n in range(2)]
        hf = [at(f"hf{n}", [128, CAP], F32, o_vn + 2048 + n * 1024) for n in range(2)]
        hh = [at(f"hh{n}", [128, CAP], F32R, o_vn + 4096 + n * 1024) for n in range(2)]
        hl = [at(f"hl{n}", [128, CAP], F32R, o_vn + 6144 + n * 1024) for n in range(2)]
        ys = at("ys", [128, 2, D], F32, o_e)

        T = [pb(f"T{n}") for n in range(3)]
        PJ = [pb(f"PJ{n}") for n in range(2)]
        SC = [pb(f"SC{n}") for n in range(2)]
        R = pb("R")

        x_in = [sem(f"x_in{n}") for n in range(2)]
        w_in = [sem(f"w_in{n}") for n in range(4)]
        gw_in = sem("gw_in")
        ctx_in = [sem(f"ctx_in{a}") for a in range(2)]
        zeroed = sem("zeroed")
        x2_out = sem("x2_out")
        scattered = [sem(f"scattered{a}") for a in range(2)]
        row_free = [sem(f"row_free{a}") for a in range(2)]
        const_ready = sem("const_ready")
        const_step = sem("const_step")
        w_T, w_hi, w_lo = sem("w_T"), sem("w_hi"), sem("w_lo")
        gw_T, gw_ok = sem("gw_T"), sem("gw_ok")
        x_stat, x_rstd, x_norm = sem("x_stat"), sem("x_rstd"), sem("x_norm")
        x_T, x_hi, x_lo = sem("x_T"), sem("x_hi"), sem("x_lo")
        pj, pj_hi, pj_lo = sem("pj"), sem("pj_hi"), sem("pj_lo")
        c_T, c_hi, c_lo = sem("c_T"), sem("c_hi"), sem("c_lo")
        v_hi, v_lo = sem("v_hi"), sem("v_lo")
        vn_mm, vn_hi, vn_lo = sem("vn_mm"), sem("vn_hi"), sem("vn_lo")
        scores, negmax, expd, sum_inv = sem("scores"), sem("negmax"), sem("expd"), sem("sum_inv")
        a_T, a_hi, a_lo = sem("a_T"), sem("a_hi"), sem("a_lo")
        attn, attn_out = sem("attn"), sem("attn_out")
        o_T, o_hi, o_lo = sem("o_T"), sem("o_hi"), sem("o_lo")
        wo_mm, x2_ok = sem("wo_mm"), sem("x2_ok")
        x2_stat, x2_rstd, x2_norm, x2_copy = sem("x2_stat"), sem("x2_rstd"), sem("x2_norm"), sem("x2_copy")
        x2_T, x2_Tok = sem("x2_T"), sem("x2_Tok")
        logits, masked, prefix, rows_ok = sem("logits"), sem("masked"), sem("prefix"), sem("rows_ok")
        gap_ready, gap_exp = sem("gap_ready"), sem("gap_exp")
        total, most_ok = sem("total"), sem("most_ok")
        vchain = sem("vchain")
        pchain = sem("pchain")

        ZR = 2
        ZN = (RROWS + 2 * CAP) // (128 * ZR)
        ZF = (ROWS - RROWS) // (128 * ZR)

        block = stack.enter_context(nc.Block())

        def hl_matmul(o, lh, ll, rh, rl, n, start=True, stop=True):
            last = None
            for k in range(n):
                first = start and k == 0
                end = stop and k == n - 1
                nc.tensor.matmul(o, lh(k), rh(k), start=first, stop=False)
                nc.tensor.matmul(o, lh(k), rl(k), start=False, stop=False)
                last = nc.tensor.matmul(o, ll(k), rh(k), start=False, stop=end)
            return last

        def transposes(bank, blocks, rows=None):
            last = None
            for col, src, p, f in blocks:
                last = nc.tensor.transpose(bank[0:f, col:col + p], src, ident[0:p, 0:p])
            return last

        def pe_w(pe, n, k, bank):
            if k == 0:
                pe.wait_ge(w_in[n], 16)
            transposes(bank, [(128 * r, wnat[n % 2][:, r, 128 * k:128 * k + 128], 128, 128)
                              for r in range(KT)]).then_inc(w_T, 1)

        def pe_xT(pe, g, a, bank):
            pe.wait_ge(x_norm, g + 1)
            transposes(bank, [(S * k, xn[a][:, 128 * k:128 * k + 128], S, 128)
                              for k in range(KT)]).then_inc(x_T, 1)

        def pe_proj(pe, p, c, bank):
            w = c // 2
            for h in range(2):
                m = 2 * (c % 2) + h
                last = hl_matmul(bank[:, h * 2 * S:(h + 1) * 2 * S],
                                 lambda k: wTh[w][:, k, 128 * m:128 * m + 128],
                                 lambda k: wTl[w][:, k, 128 * m:128 * m + 128],
                                 lambda k: xTh[:, k, :], lambda k: xTl[:, k, :], KT)
            last.then_inc(pj, 1)

        def pe_cT(pe, g, a, k, bank):
            blocks = []
            col = 0
            for j, n in enumerate(CROWS):
                blocks.append((col, cn[a][0:n, j, 128 * k:128 * k + 128], n, 128))
                col += n
            transposes(bank, blocks).then_inc(c_T, 1)

        def pe_vnew(pe, a, bank):
            hl_matmul(bank[0:S, :], lambda k: xTh[:, k, a * S:a * S + S], lambda k: xTl[:, k, a * S:a * S + S],
                      lambda k: wTh[2][:, k, :], lambda k: wTl[2][:, k, :], KT).then_inc(vn_mm, 1)

        def pe_scores(pe, a):
            hl_matmul(SC[a][0:S, 0:KP], lambda k: qTh[:, k, a * S:a * S + S], lambda k: qTl[:, k, a * S:a * S + S],
                      lambda k: kTh[:, k, a, :], lambda k: kTl[:, k, a, :], KT).then_inc(scores, 1)

        def pe_aT(pe, g, a, bank):
            pe.wait_ge(expd, g + 1)
            transposes(bank, [(S * j, ex[a][:, c:c + 128], S, 128)
                              for j, c in enumerate((0, S, S + 128, S + 256))]).then_inc(a_T, 1)

        def pe_attn(pe, g, a, bank):
            pe.wait_ge(a_lo, g + 1)
            pe.wait_ge(vn_lo, g + 1)
            o = bank[0:S, :]
            nc.tensor.matmul(o, aTh[0:S, 0, :], vnh[a][:, :], start=True, stop=False)
            nc.tensor.matmul(o, aTh[0:S, 0, :], vnl[a][:, :], start=False, stop=False)
            nc.tensor.matmul(o, aTl[0:S, 0, :], vnh[a][:, :], start=False, stop=False)
            for j, n in enumerate(CROWS):
                pe.wait_ge(v_lo, 3 * g + j + 1)
                nc.tensor.matmul(o, aTh[0:n, j + 1, :], vh[a][0:n, j, :], start=False, stop=False)
                nc.tensor.matmul(o, aTh[0:n, j + 1, :], vl[a][0:n, j, :], start=False, stop=False)
                last = nc.tensor.matmul(o, aTl[0:n, j + 1, :], vh[a][0:n, j, :], start=False, stop=j == 2)
            last.then_inc(attn, 1)

        def pe_oT(pe, g, bank):
            pe.wait_ge(attn_out, g + 1)
            transposes(bank, [(S * k, on[:, 128 * k:128 * k + 128], S, 128)
                              for k in range(KT)]).then_inc(o_T, 1)

        def pe_wo(pe, g, bank):
            pe.wait_ge(o_lo, g + 1)
            hl_matmul(bank[0:S, :], lambda k: oTh[:, k, :], lambda k: oTl[:, k, :],
                      lambda k: wTh[3][:, k, :], lambda k: wTl[3][:, k, :], KT).then_inc(wo_mm, 1)

        def pe_x2T(pe, g, a, bank):
            pe.wait_ge(x2_norm, g + 1)
            transposes(bank, [(S * k, xr[a][:, 0, 128 * k:128 * k + 128], S, 128)
                              for k in range(KT)]).then_inc(x2_T, 1)

        def pe_logits(pe, g, a):
            pe.wait_ge(x2_Tok, g + 1)
            for k in range(KT):
                last = nc.tensor.matmul(R[0:S, 8 * a:8 * a + 8], x2T[:, k, :], gwT[:, k, :],
                                        start=k == 0, stop=k == KT - 1)
            last.then_inc(logits, 1)

        def pe_prefix(pe, g, a):
            pe.wait_ge(masked, g + 1)
            o = R[0:S, 16 + 8 * a:24 + 8 * a]
            nc.tensor.matmul(o, tri[:, :], mboth[:, a, :], start=True, stop=False)
            nc.tensor.matmul(o, ones[:, :], msum[:, 1 - a, :], start=False, stop=True).then_inc(prefix, 1)

        m_in = [sem(f"m_in{n}") for n in range(NG)]
        d_in = [sem(f"d_in{n}") for n in range(2)]
        xe_in = [sem(f"xe_in{n}") for n in range(2)]
        mg_T, mg_hi, mg_lo = sem("mg_T"), sem("mg_hi"), sem("mg_lo")
        md_T, md_hi, md_lo = sem("md_T"), sem("md_hi"), sem("md_lo")
        e_T, e_hi, e_lo = sem("e_T"), sem("e_hi"), sem("e_lo")
        gu_mm, silu_ok, h_ok = sem("gu_mm"), sem("silu_ok"), sem("h_ok")
        y_mm, y_ok, yidx_ok = sem("y_mm"), sem("y_ok"), sem("yidx_ok")
        y_added, y_free = sem("y_added"), sem("y_free")
        o_zero, o_scat, o_xe, o_eT, o_hi2, o_lo2 = (sem("o_zero"), sem("o_scat"), sem("o_xe"), sem("o_eT"),
                                                    sem("o_hi2"), sem("o_lo2"))
        UB = 2 * IT

        def wtile(u, w, h):
            return wt[u % 2][2 * w + h]

        def pe_mT(pe, it, u, ws=(0, 1)):
            n = u % NG
            pe.wait_ge(m_in[n], 16 * (it * (UB // NG) + u // NG + 1))
            for w in ws:
                if u:
                    pe.wait_ge(mg_lo, 2 * (it * UB + u) - 1 + w)
                transposes(T[w], [(128 * k, ng[n][:, w, 128 * k:128 * k + 128], 128, 128)
                                  for k in range(KT)]).then_inc(mg_T, 1)

        def pe_dT(pe, it, u):
            e = u // IT
            i = u % IT
            if i == 0:
                pe.wait_ge(d_in[e], 16 * (it + 1))
            if u:
                pe.wait_ge(md_lo, it * UB + u)
            transposes(T[2], [(128 * r, dn[e][:, r, 128 * i:128 * i + 128], 128, 128)
                              for r in range(KT)]).then_inc(md_T, 1)

        def pe_eT(pe, it, e, t, sems):
            transposes(R, [(128 * k, xe[e][:, t, 128 * k:128 * k + 128], 128, 128)
                           for k in range(KT)]).then_inc(sems, 1)

        def pe_gu(pe, it, u):
            e = u // IT
            pe.wait_ge(mg_lo, 2 * (it * UB + u) + 2)
            if u % IT == 0:
                pe.wait_ge(e_lo, 2 * (2 * it + e) + 2)
            for w in range(2):
                last = hl_matmul(PJ[u % 2][:, w * CAP:(w + 1) * CAP],
                                 lambda k: wtile(u, w, 0)[:, 128 * k:128 * k + 128],
                                 lambda k: wtile(u, w, 1)[:, 128 * k:128 * k + 128],
                                 lambda k: eh[e][:, k, :], lambda k: el_[e][:, k, :], KT)
            last.then_inc(gu_mm, 1)

        def pe_down(pe, it, u):
            e, i = u // IT, u % IT
            pe.wait_ge(h_ok, it * UB + u + 1)
            pe.wait_ge(md_lo, it * UB + u + 1)
            if u == IT:
                pe.wait_ge(y_ok, 4 * it + 2)
            b = u % 2
            for t in range(2):
                o = SC[t][:, :]
                s = slice(128 * t, 128 * t + 128)
                nc.tensor.matmul(o, hh[b][:, s], wtile(u, 2, 0)[:, :], start=i == 0, stop=False)
                nc.tensor.matmul(o, hh[b][:, s], wtile(u, 2, 1)[:, :], start=False, stop=False)
                last = nc.tensor.matmul(o, hl[b][:, s], wtile(u, 2, 0)[:, :], start=False, stop=i == IT - 1)
            last.then_inc(y_mm, 1)

        def pe_experts(pe, it):
            for u in range(UB):
                e, i = u // IT, u % IT
                pe_mT(pe, it, u + 1)
                pe_dT(pe, it, u)
                if i == 3 or i == 6:
                    t = i // 6
                    nxt = 2 * it + e + 1
                    if t == 0:
                        pe.wait_ge(xe_in[(e + 1) % 2], 16 * (it + e + 1))
                    pe.wait_ge(e_lo, 2 * nxt + t)
                    pe_eT(pe, it, (e + 1) % 2, t, e_T)
                pe_gu(pe, it, u)
                if u:
                    pe_down(pe, it, u - 1)
            pe_down(pe, it, UB - 1)

        @block.tensor
        def _(pe):
            pe.wait_ge(const_ready, 1)
            for k in range(KT):
                if k == 3:
                    pe.wait_ge(w_lo, 1)
                pe_w(pe, 0, k, T[k % 3])
            pe.wait_ge(w_lo, 2)
            pe_xT(pe, 0, 0, T[1])
            pe.wait_ge(w_lo, 3)
            pe_xT(pe, 1, 1, T[2])
            pe.wait_ge(w_lo, 4)
            pe_w(pe, 1, 0, T[0])
            pe.wait_ge(x_lo, 2)
            pe_proj(pe, 0, 0, PJ[0])
            pe_w(pe, 1, 1, T[1])
            pe_w(pe, 1, 2, T[2])
            pe_proj(pe, 0, 1, PJ[1])
            pe.wait_ge(w_lo, 5)
            pe_w(pe, 1, 3, T[0])
            pe.wait_ge(w_lo, 8)
            pe.wait_ge(pj_lo, 1)
            pe_proj(pe, 0, 2, PJ[0])
            pe_w(pe, 2, 0, T[1])
            pe_w(pe, 2, 1, T[2])
            pe.wait_ge(pj_lo, 2)
            pe_proj(pe, 0, 3, PJ[1])
            pe_w(pe, 2, 2, T[0])
            pe.wait_ge(w_lo, 9)
            pe_w(pe, 2, 3, T[1])
            pe.wait_ge(gw_in, 16)
            transposes(R, [(8 * k, gwn[:, 128 * k:128 * k + 128], NE, 128) for k in range(KT)]).then_inc(gw_T, 1)
            pe.wait_ge(ctx_in[0], 32)
            pe.wait_ge(w_lo, 11)
            pe_cT(pe, 0, 0, 0, T[0])
            pe_w(pe, 3, 0, SC[1])
            pe.wait_ge(w_lo, 12)
            pe_cT(pe, 0, 0, 1, T[1])
            pe_cT(pe, 0, 0, 2, T[2])
            pe.wait_ge(c_lo, 1)
            pe_cT(pe, 0, 0, 3, T[0])
            pe.wait_ge(gw_ok, 1)
            pe_w(pe, 3, 1, R)
            pe.wait_ge(pj_lo, 3)
            pe_vnew(pe, 0, PJ[0])
            pe.wait_ge(w_lo, 13)
            pe_w(pe, 3, 2, SC[1])
            pe.wait_ge(ctx_in[1], 32)
            pe.wait_ge(c_lo, 2)
            pe_cT(pe, 1, 1, 0, T[1])
            pe.wait_ge(c_lo, 3)
            pe_cT(pe, 1, 1, 1, T[2])
            pe.wait_ge(w_lo, 14)
            pe_w(pe, 3, 3, R)
            pe.wait_ge(pj_lo, 4)
            pe.wait_ge(c_lo, 4)
            pe_scores(pe, 0)
            pe_cT(pe, 1, 1, 2, T[0])
            pe.wait_ge(w_lo, 16)
            pe.wait_ge(c_lo, 5)
            pe_cT(pe, 1, 1, 3, T[1])

            def body(p, more):
                A, B, NA = 2 * p, 2 * p + 1, 2 * p + 2
                pe_vnew(pe, 1, PJ[1])
                pe.wait_ge(c_lo, 4 * B + 3)
                pe_aT(pe, A, 0, T[0])
                pe.wait_ge(c_lo, 4 * B + 4)
                pe_scores(pe, 1)
                pe_attn(pe, A, 0, PJ[0])
                pe_aT(pe, B, 1, T[1])
                if more:
                    pe_xT(pe, NA, 0, T[2])
                    pe_xT(pe, NA + 1, 1, T[0])
                pe_oT(pe, A, SC[0])
                pe_attn(pe, B, 1, PJ[1])
                pe_wo(pe, A, PJ[0])
                pe_oT(pe, B, SC[1])
                if more:
                    pe.wait_ge(x_lo, NA + 2)
                    pe_proj(pe, p + 1, 0, PJ[1])
                pe.wait_ge(x2_ok, A + 1)
                pe_wo(pe, B, PJ[0])
                pe_x2T(pe, A, 0, T[1])
                if more:
                    pe.wait_ge(pj_lo, 4 * p + 5)
                    pe_proj(pe, p + 1, 1, PJ[1])
                else:
                    pe_mT(pe, 0, 0, (0,))
                pe_logits(pe, A, 0)
                if not more:
                    pe_mT(pe, 0, 0, (1,))
                pe_x2T(pe, B, 1, T[2])
                if more:
                    pe.wait_ge(x2_ok, B + 1)
                    pe_proj(pe, p + 1, 2, PJ[0])
                pe_prefix(pe, A, 0)
                pe_logits(pe, B, 1)
                if more:
                    pe.wait_ge(ctx_in[0], 32 * p + 64)
                    pe_cT(pe, NA, 0, 0, T[0])
                    pe_cT(pe, NA, 0, 1, T[1])
                    pe.wait_ge(pj_lo, 4 * p + 6)
                    pe_proj(pe, p + 1, 3, PJ[1])
                    pe_cT(pe, NA, 0, 2, T[2])
                    pe.wait_ge(c_lo, 4 * NA + 1)
                    pe_cT(pe, NA, 0, 3, T[0])
                pe_prefix(pe, B, 1)
                if more:
                    pe.wait_ge(pj_lo, 4 * p + 7)
                    pe_vnew(pe, 0, PJ[0])
                    pe.wait_ge(ctx_in[1], 32 * p + 64)
                    pe.wait_ge(c_lo, 4 * NA + 2)
                    pe_cT(pe, NA + 1, 1, 0, T[1])
                    pe.wait_ge(c_lo, 4 * NA + 3)
                    pe_cT(pe, NA + 1, 1, 1, T[2])
                    pe.wait_ge(pj_lo, 4 * p + 8)
                    pe.wait_ge(c_lo, 4 * NA + 4)
                    pe_scores(pe, 0)
                    pe_cT(pe, NA + 1, 1, 2, T[0])
                    pe.wait_ge(c_lo, 4 * NA + 5)
                    pe_cT(pe, NA + 1, 1, 3, T[1])

            with pe.Fori(0, PAIRS - 1) as p:
                body(p, True)
            body(PAIRS - 1, False)

            pe.wait_ge(rows_ok, NB)
            nc.tensor.matmul(R[0:S, 0:8], ones[:, :], msum[:, 1, :], start=True, stop=True).then_inc(total, 1)

            pe.wait_ge(most_ok, 1)
            pe.wait_ge(xe_in[0], 16)
            pe_eT(pe, 0, 0, 0, e_T)
            pe.wait_ge(e_lo, 1)
            pe_eT(pe, 0, 0, 1, e_T)
            with pe.Fori(0, NE // 2) as j:
                pe_experts(pe, j)
            longest = pe.value_load(mosti[0:1, 0:1], min_val=0, max_val=TOK)
            with pe.If(longest > CAP):
                pe.wait_ge(e_lo, 2 * NE + 2)
                pe.wait_ge(o_xe, 16)
                pe_eT(pe, 0, 0, 0, o_eT)
                pe.wait_ge(o_lo2, 1)
                pe_eT(pe, 0, 0, 1, o_eT)
                pe.wait_ge(o_lo2, 2)
                with pe.Fori(NE // 2, ROUNDS * NE // 2) as j:
                    pe_experts(pe, j)

        @block.scalar
        def _(act):
            def copy(o, i, s, n=1):
                nc.scalar.activation(o, i, ACT.Copy).then_inc(s, n)

            def hi_w(n, k, bank):
                act.wait_ge(w_T, 4 * n + k + 1)
                copy(wTh[n][:, k, :], bank[:, :], w_hi)

            def hi_x(g, a, bank):
                act.wait_ge(x_T, g + 1)
                copy(xTh[:, :, a * S:a * S + S], bank[:, 0:KT * S].rearrange("p (k t) -> p k t", k=KT), x_hi)

            def hi_pj(n, c, bank):
                act.wait_ge(pj, n)
                v = bank[:, 0:4 * S].rearrange("p (m t) -> p m t", m=2)
                m = 2 * (c % 2)
                if c < 2:
                    copy(qTh[:, m:m + 2, :], v, pj_hi)
                else:
                    copy(kTh[:, m:m + 2, :, 0:S], v.rearrange("p m (a t) -> p m a t", a=2), pj_hi)

            def hi_c(g, a, k):
                act.wait_ge(c_T, 4 * g + k + 1)
                copy(kTh[:, k, a, CTX:KEYS], T[(k + a) % 3][:, 0:C], c_hi)

            def hi_vn(g, a, bank):
                act.wait_ge(vn_mm, g + 1)
                copy(vnh[a][:, :], bank[0:S, :], vn_hi)

            def hi_v(a, uses):
                act.wait_ge(ctx_in[a], 32 * uses)
                for j, n in enumerate(CROWS):
                    copy(vh[a][0:n, j, :], cn[a][0:n, j, :], v_hi)

            def do_exp(g, a):
                act.wait_ge(negmax, g + 1)
                nc.scalar.activation(ex[a][:, 0:KEYS], SC[a][0:S, 0:KEYS], ACT.Exp, bias=nm[:, a, :],
                                     scale=SCALE, accum_out=esum[:, a, :]).then_inc(expd, 1)

            def hi_a(g, bank):
                act.wait_ge(a_T, g + 1)
                copy(aTh[:, :, :], bank[:, 0:4 * S].rearrange("p (k t) -> p k t", k=4), a_hi)

            def do_o(g, a, bank):
                act.wait_ge(attn, g + 1)
                act.wait_ge(sum_inv, g + 1)
                nc.scalar.activation(on[:, :], bank[0:S, :], ACT.Copy, scale=rinv[:, a, :]).then_inc(attn_out, 1)

            def hi_o(g, bank):
                act.wait_ge(o_T, g + 1)
                copy(oTh[:, :, :], bank[:, 0:4 * S].rearrange("p (k t) -> p k t", k=4), o_hi)

            def keep_x2(g, a):
                act.wait_ge(x2_norm, g + 1)
                copy(xr[a][:, 1, 0:D], xr[a][:, 0, 0:D], x2_copy)
                copy(xn2_all[:, g, :], xr[a][:, 0, 0:D], x2_copy)

            def x2T_out(g, bank):
                act.wait_ge(x2_T, g + 1)
                copy(x2T[:, :, :], bank[:, 0:4 * S].rearrange("p (k t) -> p k t", k=4), x2_Tok)

            def gap(g, a):
                act.wait_ge(gap_ready, g + 1)
                nc.scalar.activation(el[:, a, :], dl[:, a, :], ACT.Exp).then_inc(gap_exp, 1)

            for k in range(KT):
                hi_w(0, k, T[k % 3])
            hi_x(0, 0, T[1])
            hi_x(1, 1, T[2])
            hi_w(1, 0, T[0])
            hi_pj(1, 0, PJ[0])
            hi_w(1, 1, T[1])
            hi_w(1, 2, T[2])
            hi_pj(2, 1, PJ[1])
            hi_w(1, 3, T[0])
            hi_pj(3, 2, PJ[0])
            hi_w(2, 0, T[1])
            hi_w(2, 1, T[2])
            hi_pj(4, 3, PJ[1])
            hi_w(2, 2, T[0])
            hi_w(2, 3, T[1])
            hi_c(0, 0, 0)
            hi_w(3, 0, SC[1])
            for k in range(1, KT):
                hi_c(0, 0, k)
            hi_w(3, 1, R)
            hi_v(0, 1)
            hi_vn(0, 0, PJ[0])
            hi_w(3, 2, SC[1])
            hi_c(1, 1, 0)
            hi_c(1, 1, 1)
            hi_w(3, 3, R)
            hi_v(1, 1)
            hi_c(1, 1, 2)
            hi_c(1, 1, 3)

            def body(p, more):
                A, B, NA = 2 * p, 2 * p + 1, 2 * p + 2
                do_exp(A, 0)
                hi_vn(B, 1, PJ[1])
                hi_a(A, T[0])
                do_exp(B, 1)
                do_o(A, 0, PJ[0])
                hi_a(B, T[1])
                if more:
                    hi_x(NA, 0, T[2])
                    hi_x(NA + 1, 1, T[0])
                hi_o(A, SC[0])
                do_o(B, 1, PJ[1])
                hi_o(B, SC[1])
                if more:
                    hi_pj(4 * p + 5, 0, PJ[1])
                keep_x2(A, 0)
                x2T_out(A, T[1])
                if more:
                    hi_pj(4 * p + 6, 1, PJ[1])
                else:
                    hi_m(0, 0)
                x2T_out(B, T[2])
                keep_x2(B, 1)
                gap(A, 0)
                if more:
                    hi_pj(4 * p + 7, 2, PJ[0])
                    hi_c(NA, 0, 0)
                    hi_c(NA, 0, 1)
                    hi_pj(4 * p + 8, 3, PJ[1])
                    hi_c(NA, 0, 2)
                    hi_c(NA, 0, 3)
                gap(B, 1)
                if more:
                    hi_v(0, p + 2)
                    hi_vn(NA, 0, PJ[0])
                    hi_c(NA + 1, 1, 0)
                    hi_c(NA + 1, 1, 1)
                    hi_v(1, p + 2)
                    hi_c(NA + 1, 1, 2)
                    hi_c(NA + 1, 1, 3)

            def hi_m(it, u):
                for w in range(2):
                    act.wait_ge(mg_T, 2 * (it * UB + u) + 1 + w)
                    copy(wtile(u, w, 0)[:, :], T[w][:, :], mg_hi)

            def hi_e(n, e, t, tr, done):
                act.wait_ge(tr, n)
                copy(eh[e][:, :, 128 * t:128 * t + 128], R[:, :].rearrange("p (k s) -> p k s", k=KT), done)

            def y_out(it, e):
                act.wait_ge(y_mm, it * UB + IT * (e + 1))
                act.wait_ge(y_free, 2 * it + e + 1)
                for t in range(2):
                    nc.scalar.activation(ys[:, t, :], SC[t][:, :], ACT.Copy,
                                         scale=xe[e][:, t, D:D + 1]).then_inc(y_ok, 1)

            def experts(it):
                for u in range(UB):
                    e, i = u // IT, u % IT
                    hi_m(it, u + 1)
                    act.wait_ge(md_T, it * UB + u + 1)
                    copy(wtile(u, 2, 0)[:, :], T[2][:, :], md_hi)
                    if i == 3 or i == 6:
                        hi_e(2 * (2 * it + e + 1) + 1 + i // 6, (e + 1) % 2, i // 6, e_T, e_hi)
                    act.wait_ge(gu_mm, it * UB + u + 1)
                    nc.scalar.activation(hs[u % 2][:, :], PJ[u % 2][:, 0:CAP], ACT.Silu).then_inc(silu_ok, 1)
                    if i == 0 and e == 1:
                        y_out(it, 0)
                y_out(it, 1)

            with act.Fori(0, PAIRS - 1) as p:
                body(p, True)
            body(PAIRS - 1, False)
            hi_e(1, 0, 0, e_T, e_hi)
            hi_e(2, 0, 1, e_T, e_hi)
            with act.Fori(0, NE // 2) as j:
                experts(j)
            act.wait_ge(most_ok, 1)
            longest = act.value_load(mosti[0:1, 0:1], min_val=0, max_val=TOK)
            with act.If(longest > CAP):
                hi_e(1, 0, 0, o_eT, o_hi2)
                hi_e(2, 0, 1, o_eT, o_hi2)
                with act.Fori(NE // 2, ROUNDS * NE // 2) as j:
                    experts(j)

        @block.vector
        def _(dve):
            v = nc.vector
            def lo(o, psum, hi, s):
                v.tensor_tensor(o, psum, hi.bitcast(F32), ALU.subtract).then_inc(s, 1)

            chain = [0, 0]

            def link(ins, plain=False):
                ins.then_inc(vchain, 1)
                chain[1] += 1
                dve.wait_ge(vchain, chain[0] + chain[1])
                if plain:
                    met()

            def met():
                v.memset(spare[0:1, 0:1], 0.0)

            def lo_w(n, k, bank):
                dve.wait_ge(w_hi, 4 * n + k + 1)
                lo(wTl[n][:, k, :], bank[:, :], wTh[n][:, k, :], w_lo)

            def stat_x(g, a):
                link(v.bn_stats(st[:, a, :], x_all[:, g, :]), plain=True)
                link(v.bn_aggr(mv1[:, a, :], st[:, a, :]))
                v.tensor_scalar(ve1[:, a, :], mv1[:, a, 1:2], EPS, None, ALU.add).then_inc(x_stat, 1)

            def norm_x(g, a):
                dve.wait_ge(x_rstd, g + 1)
                v.tensor_scalar(xn[a][:, :], x_all[:, g, :], mv1[:, a, 0:1], rs1[:, a, :],
                                ALU.subtract, ALU.mult).then_inc(x_norm, 1)

            def lo_x(g, a, bank):
                dve.wait_ge(x_hi, g + 1)
                lo(xTl[:, :, a * S:a * S + S], bank[:, 0:KT * S].rearrange("p (k t) -> p k t", k=KT),
                   xTh[:, :, a * S:a * S + S], x_lo)

            def lo_pj(n, c, bank):
                dve.wait_ge(pj_hi, n)
                w = bank[:, 0:4 * S].rearrange("p (m t) -> p m t", m=2)
                m = 2 * (c % 2)
                if c < 2:
                    lo(qTl[:, m:m + 2, :], w, qTh[:, m:m + 2, :], pj_lo)
                else:
                    lo(kTl[:, m:m + 2, :, 0:S], w.rearrange("p m (a t) -> p m a t", a=2),
                       kTh[:, m:m + 2, :, 0:S], pj_lo)

            def lo_c(g, a, k):
                dve.wait_ge(c_hi, 4 * g + k + 1)
                lo(kTl[:, k, a, CTX:KEYS], T[(k + a) % 3][:, 0:C], kTh[:, k, a, CTX:KEYS], c_lo)

            def lo_vn(g, a, bank):
                dve.wait_ge(vn_hi, g + 1)
                lo(vnl[a][:, :], bank[0:S, :], vnh[a][:, :], vn_lo)

            def do_max(g, a):
                dve.wait_ge(scores, g + 1)
                link(v.reduce_max(mx[:, a, :], SC[a][0:S, 0:KEYS], AX.X))
                v.tensor_scalar(nm[:, a, :], mx[:, a, :], -SCALE, None, ALU.mult).then_inc(negmax, 1)

            def inv(g, a):
                dve.wait_ge(expd, g + 1)
                v.reciprocal(rinv[:, a, :], esum[:, a, :]).then_inc(sum_inv, 1)

            def lo_a(g, bank):
                dve.wait_ge(a_hi, g + 1)
                lo(aTl[:, :, :], bank[:, 0:4 * S].rearrange("p (k t) -> p k t", k=4), aTh[:, :, :], a_lo)

            def lo_o(g, bank):
                dve.wait_ge(o_hi, g + 1)
                lo(oTl[:, :, :], bank[:, 0:4 * S].rearrange("p (k t) -> p k t", k=4), oTh[:, :, :], o_lo)

            def x2_stats(g, a):
                dve.wait_ge(wo_mm, g + 1)
                v.tensor_tensor(x_all[:, g, :], PJ[0][0:S, :], x_all[:, g, :], ALU.add).then_inc(x2_ok, 1)
                dve.wait_ge(x2_ok, g + 1)
                met()
                link(v.bn_stats(st2[:, a, :], x_all[:, g, :]), plain=True)
                link(v.bn_aggr(mv2[:, a, :], st2[:, a, :]))
                v.tensor_scalar(ve2[:, a, :], mv2[:, a, 1:2], EPS, None, ALU.add).then_inc(x2_stat, 1)

            def x2_norms(g, a, used):
                dve.wait_ge(x2_rstd, g + 1)
                dve.wait_ge(row_free[a], used)
                v.tensor_scalar(xr[a][:, 0, 0:D], x_all[:, g, :], mv2[:, a, 0:1], rs2[:, a, :],
                                ALU.subtract, ALU.mult).then_inc(x2_norm, 1)

            def topk(g, a):
                dve.wait_ge(logits, g + 1)
                if a:
                    dve.wait_ge(prefix, g)
                    v.tensor_copy(pos[:, 0, :], R[0:S, 16:24])
                link(v.tensor_copy(lgs[:, a, :], R[0:S, 8 * a:8 * a + 8]), plain=True)
                link(v.max(mx8[:, a, :], lgs[:, a, :]), plain=True)
                link(v.max_index(ix8[:, a, :], mx8[:, a, :], lgs[:, a, :]))
                link(v.tensor_copy(ixf[:, a, :], ix8[:, a, 0:2]))
                v.tensor_scalar(mask[:, a, 0, :], iota8[:, :], ixf[:, a, 0:1], None, ALU.is_equal)
                link(v.tensor_scalar(mask[:, a, 1, :], iota8[:, :], ixf[:, a, 1:2], None, ALU.is_equal))
                v.tensor_tensor(mboth[:, a, :], mask[:, a, 0, :], mask[:, a, 1, :], ALU.add).then_inc(masked, 1)
                v.tensor_tensor(dl[:, a, :], mx8[:, a, 1:2], mx8[:, a, 0:1], ALU.subtract).then_inc(gap_ready, 1)
                dve.wait_ge(masked, g + 1)
                link(v.tensor_tensor(msum[:, a, :], msum[:, 1 - a, :], mboth[:, a, :], ALU.add))

            def rows(g, a):
                dve.wait_ge(gap_exp, g + 1)
                link(v.tensor_scalar(el1[:, a, :], el[:, a, :], 1.0, None, ALU.add))
                link(v.reciprocal(wts[:, a, 0:1], el1[:, a, :]))
                link(v.tensor_tensor(wts[:, a, 1:2], el[:, a, :], wts[:, a, 0:1], ALU.mult))
                v.tensor_copy(w_all[:, g, :], wts[:, a, :])
                v.tensor_copy(xr[a][:, :, D], wts[:, a, :])
                v.tensor_scalar(xr[a][:, :, D + 1], xr[a][:, :, D + 1], 2.0 * S, None, ALU.add)
                if a:
                    dve.wait_ge(prefix, g + 1)
                    link(v.tensor_copy(pos[:, 1, :], R[0:S, 24:32]))
                v.tensor_tensor(rb[:, a, :], pos[:, a, :], ebase[:, :], ALU.add)
                link(v.tensor_scalar(rr[:, a, :], pos[:, a, :], float(CAP), None, ALU.is_ge))
                link(v.scalar_tensor_tensor(rr2[:, a, :], pos[:, a, :], 2.0 * CAP, rr[:, a, :], ALU.is_ge, ALU.add))
                link(v.scalar_tensor_tensor(rr3[:, a, :], pos[:, a, :], 3.0 * CAP, rr2[:, a, :], ALU.is_ge, ALU.add))
                link(v.scalar_tensor_tensor(row8[:, a, :], rr3[:, a, :], float(RROWS - CAP), rb[:, a, :],
                                            ALU.mult, ALU.add))
                v.tensor_tensor(junk[:, a, 0, :], row8[:, a, :], mask[:, a, 0, :], ALU.mult)
                link(v.tensor_tensor(junk[:, a, 1, :], row8[:, a, :], mask[:, a, 1, :], ALU.mult))
                link(v.reduce_sum(rowf[:, a, :], junk[:, a, :, :], AX.X))
                v.tensor_copy(idx[a][0][:, :], rowf[:, a, 0:1])
                v.tensor_copy(idx[a][1][:, :], rowf[:, a, 1:2])
                v.tensor_copy(row_all[:, g, :], rowf[:, a, :]).then_inc(rows_ok, 1)

            dve.wait_ge(const_ready, 3)
            dve.wait_ge(x_in[0], 16)
            stat_x(0, 0)
            stat_x(1, 1)
            norm_x(0, 0)
            norm_x(1, 1)
            for k in range(KT):
                lo_w(0, k, T[k % 3])
            lo_x(0, 0, T[1])
            lo_x(1, 1, T[2])
            lo_w(1, 0, T[0])
            lo_pj(1, 0, PJ[0])
            lo_w(1, 1, T[1])
            lo_w(1, 2, T[2])
            lo_pj(2, 1, PJ[1])
            lo_w(1, 3, T[0])
            lo_pj(3, 2, PJ[0])
            lo_w(2, 0, T[1])
            lo_w(2, 1, T[2])
            lo_pj(4, 3, PJ[1])
            lo_w(2, 2, T[0])
            lo_w(2, 3, T[1])
            dve.wait_ge(gw_T, 1)
            v.tensor_copy(gwT[:, :, :], R[:, 0:KT * NE].rearrange("p (k e) -> p k e", k=KT)).then_inc(gw_ok, 1)
            lo_c(0, 0, 0)
            lo_w(3, 0, SC[1])
            for k in range(1, KT):
                lo_c(0, 0, k)
            lo_w(3, 1, R)
            lo_vn(0, 0, PJ[0])
            lo_w(3, 2, SC[1])
            lo_c(1, 1, 0)
            lo_c(1, 1, 1)
            lo_w(3, 3, R)
            do_max(0, 0)
            lo_c(1, 1, 2)
            lo_c(1, 1, 3)
            dve.wait_ge(x_in[1], 16)

            def body(p, more):
                A, B, NA = 2 * p, 2 * p + 1, 2 * p + 2
                if more:
                    stat_x(NA, 0)
                    stat_x(NA + 1, 1)
                lo_vn(B, 1, PJ[1])
                inv(A, 0)
                lo_a(A, T[0])
                if more:
                    norm_x(NA, 0)
                    norm_x(NA + 1, 1)
                do_max(B, 1)
                lo_a(B, T[1])
                inv(B, 1)
                if more:
                    lo_x(NA, 0, T[2])
                    lo_x(NA + 1, 1, T[0])
                lo_o(A, SC[0])
                x2_stats(A, 0)
                lo_o(B, SC[1])
                x2_norms(A, 0, p + 1)
                if more:
                    lo_pj(4 * p + 5, 0, PJ[1])
                x2_stats(B, 1)
                x2_norms(B, 1, p + 1)
                if more:
                    lo_pj(4 * p + 6, 1, PJ[1])
                else:
                    lo_m(0, 0)
                topk(A, 0)
                if more:
                    lo_pj(4 * p + 7, 2, PJ[0])
                    lo_c(NA, 0, 0)
                    lo_c(NA, 0, 1)
                topk(B, 1)
                if more:
                    lo_pj(4 * p + 8, 3, PJ[1])
                    lo_c(NA, 0, 2)
                    lo_c(NA, 0, 3)
                rows(A, 0)
                if more:
                    lo_vn(NA, 0, PJ[0])
                    lo_c(NA + 1, 1, 0)
                    lo_c(NA + 1, 1, 1)
                rows(B, 1)
                if more:
                    do_max(NA, 0)
                    lo_c(NA + 1, 1, 2)
                    lo_c(NA + 1, 1, 3)

            def lo_m(it, u):
                for w in range(2):
                    dve.wait_ge(mg_hi, 2 * (it * UB + u) + 1 + w)
                    lo(wtile(u, w, 1)[:, :], T[w][:, :], wtile(u, w, 0)[:, :], mg_lo)

            def lo_e(n, e, t, hi, done):
                dve.wait_ge(hi, n)
                lo(el_[e][:, :, 128 * t:128 * t + 128], R[:, :].rearrange("p (k s) -> p k s", k=KT),
                   eh[e][:, :, 128 * t:128 * t + 128], done)

            def experts(it):
                for u in range(UB):
                    e, i = u // IT, u % IT
                    b = u % 2
                    lo_m(it, u + 1)
                    dve.wait_ge(md_hi, it * UB + u + 1)
                    lo(wtile(u, 2, 1)[:, :], T[2][:, :], wtile(u, 2, 0)[:, :], md_lo)
                    if i == 3 or i == 6:
                        lo_e(2 * (2 * it + e + 1) + 1 + i // 6, (e + 1) % 2, i // 6, e_hi, e_lo)
                    if i == 4:
                        link(v.scalar_tensor_tensor(yidt[:, e, :], xe[e][:, :, D + 1], 0.0, padid[:, :],
                                                    ALU.is_equal, ALU.mult))
                        v.scalar_tensor_tensor(yidx[:, e, :], xe[e][:, :, D + 1], -1.0, yidt[:, e, :],
                                               ALU.add, ALU.add).then_inc(yidx_ok, 1)
                    dve.wait_ge(silu_ok, it * UB + u + 1)
                    link(v.tensor_tensor(hf[b][:, :], PJ[b][:, CAP:2 * CAP], hs[b][:, :], ALU.mult))
                    link(v.tensor_copy(hh[b][:, :], hf[b][:, :]))
                    v.tensor_tensor(hl[b][:, :], hf[b][:, :], hh[b][:, :].bitcast(F32), ALU.subtract)\
                        .then_inc(h_ok, 1)

            def looped(first, last, f):
                before = chain[0] + chain[1]
                per = LINKS[f.__name__]
                with dve.Fori(first, last) as p:
                    chain[0], chain[1] = before + (p - first) * per, 0
                    if f is body:
                        f(p, True)
                    else:
                        f(p)
                    assert chain[1] == per, (f.__name__, chain[1])
                chain[0], chain[1] = before + (last - first) * per, 0

            LINKS = {"body": 41, "experts": 34}
            looped(0, PAIRS - 1, body)
            body(PAIRS - 1, False)
            dve.wait_ge(total, 1)
            link(v.reduce_max(most[:, 0:1], R[0:S, 0:8], AX.X))
            v.tensor_copy(mosti[:, 0:1], most[:, 0:1]).then_inc(most_ok, 1)
            lo_e(1, 0, 0, e_hi, e_lo)
            lo_e(2, 0, 1, e_hi, e_lo)
            dve.wait_ge(most_ok, 1)
            looped(0, NE // 2, experts)
            longest = dve.value_load(mosti[0:1, 0:1], min_val=0, max_val=TOK)
            with dve.If(longest > CAP):
                lo_e(1, 0, 0, o_hi2, o_lo2)
                lo_e(2, 0, 1, o_hi2, o_lo2)
                looped(NE // 2, ROUNDS * NE // 2, experts)

        @block.gpsimd
        def _(pool):
            g_ = nc.gpsimd
            g_.memset(ident[:, :], 0.0).then_inc(const_step, 1)
            pool.wait_ge(const_step, 1)
            g_.affine_select(out=ident[:, :], in_=ident[:, :], compare_op=ALU.not_equal, fill=1.0, base=0,
                             pattern=[[-1, 128]], channel_multiplier=1).then_inc(const_ready, 1)
            g_.memset(half[:, :], -0.5).then_inc(const_step, 1)
            g_.memset(zero[:, :], 0.0).then_inc(const_step, 1)
            for a in range(2):
                g_.memset(kTh[:, :, a, KEYS:KP].bitcast(F32), 0.0).then_inc(const_step, 1)
                g_.memset(kTl[:, :, a, KEYS:KP].bitcast(F32), 0.0).then_inc(const_step, 1)
                g_.memset(ex[a][:, KEYS:512], 0.0).then_inc(const_step, 1)
            g_.memset(ones[:, :], 1.0).then_inc(const_step, 1)
            g_.memset(tri[:, :], 1.0).then_inc(const_step, 1)
            g_.memset(msum[:, 1, :], 0.0).then_inc(const_step, 1)
            g_.iota(iotai[0:S, 0:8], pattern=[[1, 8]], base=0, channel_multiplier=0).then_inc(const_step, 1)
            g_.iota(iotai[0:S, 8:16], pattern=[[CAP, 8]], base=0, channel_multiplier=0).then_inc(const_step, 1)
            g_.iota(iotai[:, 16:18], pattern=[[128, 2]], base=TOK + 1, channel_multiplier=1).then_inc(const_step, 1)
            g_.iota(iotai[0:S, 18:20], pattern=[[0, 2]], base=1 - 2 * S, channel_multiplier=1)\
                .then_inc(const_step, 1)
            pool.wait_ge(const_step, 16)
            g_.affine_select(out=tri[:, :], in_=tri[:, :], compare_op=ALU.is_gt, fill=0.0, base=0,
                             pattern=[[1, S]], channel_multiplier=-1).then_inc(const_step, 1)
            g_.tensor_copy(iota8[:, :], iotai[0:S, 0:8]).then_inc(const_step, 1)
            g_.tensor_copy(ebase[:, :], iotai[0:S, 8:16]).then_inc(const_step, 1)
            g_.tensor_copy(padid[:, :], iotai[:, 16:18]).then_inc(const_step, 1)
            g_.tensor_copy(xr[0][:, :, D + 1], iotai[0:S, 18:20]).then_inc(const_step, 1)
            g_.tensor_scalar(xr[1][:, :, D + 1], iotai[0:S, 18:20], float(S), None, ALU.add).then_inc(const_step, 1)
            pool.wait_ge(const_step, 22)
            flag = [0]

            def signal(s, n=1):
                g_.memset(flags[0:1, flag[0]:flag[0] + 1], 0.0).then_inc(s, n)
                flag[0] += 1

            signal(row_free[0])
            signal(row_free[1])
            signal(y_free)
            signal(const_ready, 2)

            def power(o, i, ready, n, done):
                pool.wait_ge(ready, n)
                g_.tensor_tensor(o, i, half[0:S, 0:1], ALU.pow).then_inc(done, 1)

            def lo_v(g, a):
                pool.wait_ge(c_T, 4 * g + 4)
                for j, n in enumerate(CROWS):
                    pool.wait_ge(v_hi, 3 * g + j + 1)
                    g_.tensor_tensor(vl[a][0:n, j, :], cn[a][0:n, j, :], vh[a][0:n, j, :].bitcast(F32),
                                     ALU.subtract).then_inc(v_lo, 1)

            def scatter(g, a):
                pool.wait_ge(rows_ok, g + 1)
                pool.wait_ge(x2_copy, 2 * g + 2)
                for s in range(2):
                    pool.indirect_dma_start(slots[:, :], bass.IndirectOffsetOnAxis(idx[a][s][:, :], 0),
                                            xr[a][:, s, :], None).then_inc(scattered[a], 16)

            power(rs1[:, 0, :], ve1[:, 0, :], x_stat, 1, x_rstd)
            power(rs1[:, 1, :], ve1[:, 1, :], x_stat, 2, x_rstd)
            lo_v(0, 0)
            lo_v(1, 1)
            pool.wait_ge(zeroed, 16 * ZN)

            def body(p, more):
                A, B, NA = 2 * p, 2 * p + 1, 2 * p + 2
                if more:
                    power(rs1[:, 0, :], ve1[:, 0, :], x_stat, NA + 1, x_rstd)
                    power(rs1[:, 1, :], ve1[:, 1, :], x_stat, NA + 2, x_rstd)
                if p:
                    for a in range(2):
                        pool.wait_ge(scattered[a], 32 * p)
                        signal(row_free[a])
                power(rs2[:, 0, :], ve2[:, 0, :], x2_stat, A + 1, x2_rstd)
                power(rs2[:, 1, :], ve2[:, 1, :], x2_stat, B + 1, x2_rstd)
                if more:
                    lo_v(NA, 0)
                scatter(A, 0)
                if more:
                    lo_v(NA + 1, 1)
                scatter(B, 1)

            for p in range(PAIRS):
                body(p, p < PAIRS - 1)

            def add_y(n, e):
                pool.wait_ge(y_ok, 2 * n + 2)
                pool.wait_ge(yidx_ok, n + 1)
                for t in range(2):
                    pool.indirect_dma_start(out[:, :], bass.IndirectOffsetOnAxis(yidx[:, e, t:t + 1], 0),
                                            ys[:, t, :], None, compute_op=ALU.add).then_inc(y_added, 16)
                pool.wait_ge(y_added, 32 * n + 32)
                signal(y_free)

            pool.wait_ge(x2_out, 16 * NB + 16 * 2)
            for n in range(NE):
                add_y(n, n % 2)
            pool.wait_ge(most_ok, 1)
            longest = pool.value_load(mosti[0:1, 0:1], min_val=0, max_val=TOK)
            with pool.If(longest > CAP):
                pool.wait_ge(o_zero, 16 * ZF)
                for a in range(2):
                    g_.tensor_scalar(xr[0][:, a, D + 1:D + 2], xr[0][:, a, D + 1:D + 2], -float(TOK), None, ALU.add)\
                        .then_inc(pchain, 1)
                for g in range(NB):
                    pool.wait_ge(pchain, 2 + 7 * g)
                    if g:
                        pool.wait_ge(o_scat, 32 * g)
                    for s in range(2):
                        g_.tensor_copy(xr[0][:, s, 0:D], xn2_all[:, g, :]).then_inc(pchain, 1)
                        g_.tensor_copy(idx[0][s][:, :], row_all[:, g, s:s + 1]).then_inc(pchain, 1)
                        g_.tensor_scalar(xr[0][:, s, D + 1:D + 2], xr[0][:, s, D + 1:D + 2], float(2 * S if g == 0 else S),
                                         None, ALU.add).then_inc(pchain, 1)
                    g_.tensor_copy(xr[0][:, :, D], w_all[:, g, :]).then_inc(pchain, 1)
                    pool.wait_ge(pchain, 9 + 7 * g)
                    for s in range(2):
                        pool.indirect_dma_start(slots[:, :], bass.IndirectOffsetOnAxis(idx[0][s][:, :], 0),
                                                xr[0][:, s, :], None).then_inc(o_scat, 16)
                for n in range(NE, ROUNDS * NE):
                    add_y(n, n % 2)

        @block.sync
        def _(sp):
            xv = x.rearrange("b s d -> s b d")
            sp.dma_start(x_all[:, 0:2, :], xv[:, 0:2, :]).then_inc(x_in[0], 16)
            ws = [wq, wk, wv, wo]

            def load_w(n):
                sp.dma_start(wnat[n % 2][:, :, :], ws[n].rearrange("(r p) d -> p r d", p=128)).then_inc(w_in[n], 16)

            def load_ctx(g, a):
                sp.dma_start(cn[a][:, 0:2, :], ctxt[g, 0:256, :].rearrange("(j p) d -> p j d", p=128))\
                    .then_inc(ctx_in[a], 16)
                sp.dma_start(cn[a][0:CROWS[2], 2, :], ctxt[g, 256:C, :]).then_inc(ctx_in[a], 16)

            load_w(0)
            load_w(1)
            sp.dma_start(gwn[:, :], gate_w).then_inc(gw_in, 16)
            load_ctx(0, 0)
            sp.wait_ge(w_T, 4)
            load_w(2)
            load_ctx(1, 1)
            sp.wait_ge(w_T, 8)
            load_w(3)
            sp.dma_start(x_all[:, 2:NB, :], xv[:, 2:NB, :]).then_inc(x_in[1], 16)
            sp.wait_ge(const_step, 3)
            for n in range(ZN):
                sp.dma_start(slots[256 * n:256 * n + 256, :].rearrange("(p r) w -> p (r w)", p=128),
                             zero[:, :]).then_inc(zeroed, 16)

            def store_x2(g):
                sp.wait_ge(x2_ok, g + 1)
                sp.dma_start(out[bass.ds(g * S, S), :], x_all[:, g, :]).then_inc(x2_out, 16)

            with sp.Fori(0, PAIRS - 1) as p:
                sp.wait_ge(attn, 2 * p + 1)
                load_ctx(2 * p + 2, 0)
                sp.wait_ge(attn, 2 * p + 2)
                load_ctx(2 * p + 3, 1)
                store_x2(2 * p)
                store_x2(2 * p + 1)

            def load_m(e, i, n):
                sp.dma_start(ng[n][:, :, :],
                             gate_up.rearrange("e (w i p) d -> e i p w d", w=2, p=128)[e, i, :, :, :])\
                    .then_inc(m_in[n], 16)

            def load_d(e, par):
                sp.dma_start(dn[par][:, :, :], down.rearrange("e (r p) i -> e p r i", p=128)[e, :, :, :])\
                    .then_inc(d_in[par], 16)

            sp.wait_ge(pj, 4 * PAIRS)
            load_m(0, 0, 0)
            load_d(0, 0)
            for i in range(1, NG):
                load_m(0, i, i)
            sp.wait_ge(vn_mm, NB)
            load_d(1, 1)
            store_x2(NB - 2)
            store_x2(NB - 1)
            for n in range(2):
                sp.dma_start(out[TOK + 128 * n:TOK + 128 * n + 128, :], zero[:, 0:D]).then_inc(x2_out, 16)

            def load_xe(n, par):
                sp.dma_start(xe[par][:, :, :],
                             slots[bass.ds(n * CAP, CAP), :].rearrange("(t p) w -> p t w", p=128))\
                    .then_inc(xe_in[par], 16)

            for a in range(2):
                sp.wait_ge(scattered[a], 32 * PAIRS)
            load_xe(0, 0)
            load_xe(1, 1)

            def experts(it, e0, e2, more=True):
                for u in range(UB):
                    uu = u + NG
                    if u == IT:
                        sp.wait_ge(y_ok, 4 * it + 2)
                        sp.wait_ge(yidx_ok, 2 * it + 1)
                        load_xe(2 * it + 2, 0)
                    if u == IT + 1 and more:
                        sp.wait_ge(md_T, it * UB + IT)
                        load_d(e2, 0)
                    sp.wait_ge(mg_T, 2 * (it * UB + u) + 2)
                    if uu <= UB or more:
                        load_m(e0 + uu // IT if uu < UB else e2, uu % IT, u % NG)
                if more:
                    sp.wait_ge(md_T, it * UB + UB)
                    load_d(e2 + 1, 1)
                    sp.wait_ge(y_ok, 4 * it + 4)
                    sp.wait_ge(yidx_ok, 2 * it + 2)
                    load_xe(2 * it + 3, 1)

            with sp.Fori(0, NE // 2 - 1) as j:
                experts(j, 2 * j, 2 * j + 2)
            experts(NE // 2 - 1, NE - 2, 0, more=False)

            sp.wait_ge(most_ok, 1)
            longest = sp.value_load(mosti[0:1, 0:1], min_val=0, max_val=TOK)
            with sp.If(longest > CAP):
                sp.wait_ge(xe_in[0], 16 * (NE // 2 + 1))
                for n in range(ZF):
                    r = RROWS + 128 * ZR * n
                    sp.dma_start(slots[r:r + 128 * ZR, :].rearrange("(p r) w -> p (r w)", p=128), zero[:, :])\
                        .then_inc(o_zero, 16)
                sp.wait_ge(md_T, NE * IT)
                load_d(0, 0)
                load_d(1, 1)
                for i in range(1, NG):
                    load_m(0, i, i)
                sp.wait_ge(o_scat, 32 * NB)
                sp.wait_ge(y_ok, 2 * NE)
                sp.wait_ge(yidx_ok, NE)
                sp.wait_ge(e_T, 2 * NE + 2)
                sp.dma_start(xe[0][:, :, :], slots[RROWS:RROWS + CAP, :].rearrange("(t p) w -> p t w", p=128))\
                    .then_inc(o_xe, 16)
                load_xe(NE + 1, 1)
                with sp.Fori(1, ROUNDS) as r:
                    with sp.Fori(0, NE // 2 - 1) as j:
                        experts(r * (NE // 2) + j, 2 * j, 2 * j + 2)
                    experts(r * (NE // 2) + NE // 2 - 1, NE - 2, 0)
                for n in range(NG):
                    sp.wait_ge(m_in[n], 16 * (ROUNDS * NE * IT // NG + 1))
                for n in range(2):
                    sp.wait_ge(d_in[n], 16 * (ROUNDS * NE // 2 + 1))
                    sp.wait_ge(xe_in[n], 16 * (ROUNDS * NE // 2 + 1))


_INS = ["x", "ctx_2048", "L0_xattn_wq", "L0_xattn_wk", "L0_xattn_wv", "L0_xattn_wo", "L0_ffn_gate_weight",
        "L0_ffn_gate_up_proj", "L0_ffn_down_proj"]


def kernel(**inputs):
    import numpy as _np
    import concourse.bacc as _bacc
    from concourse import mybir as _mybir
    from concourse.bass_utils import run_bass_kernel_spmd as _run

    nc = _bacc.Bacc("TRN2", target_bir_lowering=False, num_devices=1)
    arrays, args = {}, []
    for name in _INS:
        a = _np.ascontiguousarray(inputs[name])
        arrays[f"in_{name}"] = a
        args.append(nc.dram_tensor(f"in_{name}", a.shape, _mybir.dt.from_np(a.dtype), kind="ExternalInput").ap())
    args.append(nc.dram_tensor("out", (OUTR, D), _mybir.dt.float32, kind="ExternalOutput").ap())
    build_kernel(nc, *args)
    r = _run(nc, [arrays], core_ids=[0])
    return r.results[0]["out"][0:TOK].reshape(NB, S, D)
```

```python
import concourse.bass as bass
from concourse import mybir
from contextlib import ExitStack

F32 = mybir.dt.float32
F32R = mybir.dt.float32r
BF16 = mybir.dt.bfloat16
I32 = mybir.dt.int32
U32 = mybir.dt.uint32
ACT = mybir.ActivationFunctionType
ALU = mybir.AluOpType
AX = mybir.AxisListType

NB = 8
S = 112
D = 512
KT = D // 128
C = 375
NEW = 0
CTX = S
KEYS = S + C
KP = KEYS + 1
CROWS = [128, 128, C - 256]
NE = 8
I = 1024
IT = I // 128
CAP = 256
ROUNDS = 4
RW = D + 2
RROWS = NE * CAP
ROWS = ROUNDS * RROWS
TOK = NB * S
OUTR = TOK + CAP
SCALE = float(D) ** -0.5
EPS = 1e-5
PAIRS = NB // 2
ZW = 1028


def build_kernel(nc, x, ctxt, wq, wk, wv, wo, gate_w, gate_up, down, out):
    slots = nc.dram_tensor("slots", (ROWS, RW), F32, kind="Internal").ap()

    stack = ExitStack()
    with stack:
        def sem(name):
            return stack.enter_context(nc.semaphore(name))

        def pb(name):
            return stack.enter_context(nc.psum_tensor(name, [128, 512], F32))

        top = [(nc.sbuf_base + 63) // 64 * 64]

        def at(name, shape, dt, offset):
            return nc.alloc_sbuf_tensor_at(name, shape, dt, offset=offset)

        def size(shape, dt):
            n = 1
            for s in shape[1:]:
                n *= s
            return (n * (2 if dt == BF16 else 4) + 31) // 32 * 32

        def sb(name, shape, dt):
            offset = top[0]
            top[0] += size(shape, dt)
            return at(name, shape, dt, offset)

        ident = sb("ident", [128, 128], F32)
        zero = sb("zero", [128, ZW], F32)
        tri = sb("tri", [S, S], BF16)
        ones = sb("ones", [S, S], BF16)
        iota8 = sb("iota8", [S, NE], F32)
        ebase = sb("ebase", [S, NE], F32)
        padid = sb("padid", [128, 2], F32)
        half = sb("half", [128, 8], F32)
        iotai = sb("iotai", [128, 24], I32)
        w_all = sb("w_all", [S, NB, 2], F32)
        row_all = sb("row_all", [S, NB, 2], I32)
        most = sb("most", [S, 2], F32)
        mosti = sb("mosti", [S, 2], I32)
        yidx = sb("yidx", [128, 2, 2], I32)
        spare = sb("spare", [1, 1], F32)
        flags = sb("flags", [1, 64], F32)
        yidt = sb("yidt", [128, 2, 2], F32)
        st = sb("st", [S, 2, 6], F32)
        mr_all = sb("mr_all", [S, NB, 2], F32)
        ve_all = sb("ve_all", [S, NB], F32)
        mr = sb("mr", [S, 2, 2], F32)
        st2 = sb("st2", [S, 2, 6], F32)
        mv2 = sb("mv2", [S, 2, 2], F32)
        ve2 = sb("ve2", [S, 2, 1], F32)
        rs2 = sb("rs2", [S, 2, 1], F32)
        mx = sb("mx", [S, 2, 1], F32)
        nm = sb("nm", [S, 2, 1], F32)
        esum = sb("esum", [S, 2, 1], F32)
        rinv = sb("rinv", [S, 2, 1], F32)
        lgs = sb("lgs", [S, 2, 8], F32)
        mx8 = sb("mx8", [S, 2, 8], F32)
        ix8 = sb("ix8", [S, 2, 8], U32)
        ixf = sb("ixf", [S, 2, 2], F32)
        mask = sb("mask", [S, 2, 2, 8], F32)
        mboth = sb("mboth", [S, 2, 8], BF16)
        msum = sb("msum", [S, 2, 8], BF16)
        pos = sb("pos", [S, 2, 8], F32)
        rr = sb("rr", [S, 2, 8], F32)
        rr2 = sb("rr2", [S, 2, 8], F32)
        rr3 = sb("rr3", [S, 2, 8], F32)
        rb = sb("rb", [S, 2, 8], F32)
        row8 = sb("row8", [S, 2, 8], F32)
        junk = sb("junk", [S, 2, 2, 8], F32)
        rowf = sb("rowf", [S, 2, 2], F32)
        dl = sb("dl", [S, 2, 1], F32)
        el = sb("el", [S, 2, 1], F32)
        el1 = sb("el1", [S, 2, 1], F32)
        wts = sb("wts", [S, 2, 2], F32)
        idx = [[sb(f"idx{a}{s}", [S, 1], I32) for s in range(2)] for a in range(2)]
        gwT = sb("gwT", [128, KT, NE], F32)
        o_xn2 = top[0]
        xn2_all = sb("xn2_all", [S, NB, D], F32)
        xr = [sb(f"xr{a}", [S, 2, RW], F32) for a in range(2)]

        o_w = top[0]
        wTh = [None] * 4
        wTl = [None] * 4
        for n in range(4):
            wTh[n] = sb(f"wTh{n}", [128, KT, D], F32R)
            wTl[n] = sb(f"wTl{n}", [128, KT, D], F32R)
        wnat = [at(f"wnat{n}", [128, KT, D], F32, o_xn2 + n * KT * D * 4) for n in range(2)]
        o_x = top[0]
        x_all = sb("x_all", [S, NB, D], F32)
        o_xt = top[0]
        xTh = sb("xTh", [128, KT, 2 * S], F32R)
        xTl = sb("xTl", [128, KT, 2 * S], F32R)
        qTh = sb("qTh", [128, KT, 2 * S], F32R)
        qTl = sb("qTl", [128, KT, 2 * S], F32R)
        o_keys = top[0]
        kTh = sb("kTh", [128, KT, 2, KP], F32R)
        kTl = sb("kTl", [128, KT, 2, KP], F32R)
        o_cn = top[0]
        cn = [sb(f"cn{a}", [128, 3, D], F32) for a in range(2)]
        vl = [at(f"vl{a}", [128, 3, D], F32R, o_cn + a * 3 * D * 4) for a in range(2)]
        vh = [sb(f"vh{a}", [128, 3, D], F32R) for a in range(2)]
        o_vn = top[0]
        vnh = [sb(f"vnh{a}", [S, D], F32R) for a in range(2)]
        vnl = [sb(f"vnl{a}", [S, D], F32R) for a in range(2)]
        o_e = top[0]
        ex = [sb(f"ex{a}", [S, 512], F32) for a in range(2)]
        aTh = [sb("aTh0", [128, 4, S], F32R)]
        aTl = [sb("aTl0", [128, 4, S], F32R)]
        gwn = at("gwn", [NE, D], F32, top[0])
        on = sb("on", [S, D], F32)
        oTh = [sb("oTh0", [128, KT, S], F32R)]
        oTl = [sb("oTl0", [128, KT, S], F32R)]
        oTh.append(at("oTh1", [128, KT, S], F32R, top[0]))
        oTl.append(at("oTl1", [128, KT, S], F32R, top[0] + KT * S * 4))
        xn = [sb(f"xn{a}", [S, D], F32) for a in range(2)]
        aTh.append(at("aTh1", [128, 4, S], F32R, top[0]))
        aTl.append(at("aTl1", [128, 4, S], F32R, o_e))
        x2T = sb("x2T", [128, KT, S], F32)
        assert top[0] <= nc.sbuf_usable_end, (top[0], nc.sbuf_usable_end)

        NG = 4
        ng = [at(f"ng{n}", [128, 2, D], F32, o_w + n * 4096) for n in range(NG)]
        dn = [at(f"dn{n}", [128, KT, I], F32, o_w + 16384 + n * 16384) for n in range(2)]
        GU, DU = 8, 4
        eh = [at(f"eh{n}", [128, KT, CAP], F32R, o_x + n * 8192) for n in range(2)]
        el_ = [at(f"el_{n}", [128, KT, CAP], F32R, o_x + n * 8192 + 4096) for n in range(2)]
        o_gu = [o_w + 3 * 16384 + n * 8192 for n in range(2)] + [o_xt + n * 8192 for n in range(GU - 2)]
        wgu = [[[at(f"gu{w}{h}{n}", [128, 512], F32R, o_gu[n] + (2 * w + h) * 2048) for h in range(2)]
                for w in range(2)] for n in range(GU)]
        o_d = o_xt + (GU - 2) * 8192
        wdn = [[at(f"wd{h}{n}", [128, 512], F32R, o_d + n * 4096 + h * 2048) for h in range(2)] for n in range(DU)]
        o_s = o_d + DU * 4096
        xe = [at(f"xe{n}", [128, 2, RW], F32, o_s + n * 4128) for n in range(2)]
        hs = [at(f"hs{n}", [128, CAP], F32, o_s + 8256 + n * 1024) for n in range(2)]
        hf = [at(f"hf{n}", [128, CAP], F32, o_s + 10304 + n * 1024) for n in range(2)]
        assert o_s + 12352 <= o_e
        ys = at("ys", [128, 2, D], F32, o_e)
        hh = [at(f"hh{n}", [128, CAP], F32R, o_e + 4096 + n * 1024) for n in range(2)]
        hl = [at(f"hl{n}", [128, CAP], F32R, o_e + 6144 + n * 1024) for n in range(2)]

        T = [pb(f"T{n}") for n in range(3)]
        PJ = [pb(f"PJ{n}") for n in range(2)]
        SC = [pb(f"SC{n}") for n in range(2)]
        R = pb("R")

        x_in = [sem(f"x_in{n}") for n in range(2)]
        w_in = [sem(f"w_in{n}") for n in range(4)]
        wq_half = sem("wq_half")
        gw_in = sem("gw_in")
        ctx_in = [sem(f"ctx_in{a}") for a in range(2)]
        zeroed = sem("zeroed")
        x2_out = sem("x2_out")
        scattered = [sem(f"scattered{a}") for a in range(2)]
        row_free = [sem(f"row_free{a}") for a in range(2)]
        const_ready = sem("const_ready")
        const_step = sem("const_step")
        w_T, w_hi, w_lo = sem("w_T"), sem("w_hi"), sem("w_lo")
        gw_T, gw_ok = sem("gw_T"), sem("gw_ok")
        x_stat, x_rstd, x_norm = sem("x_stat"), sem("x_rstd"), sem("x_norm")
        x_T, x_hi, x_lo = sem("x_T"), sem("x_hi"), sem("x_lo")
        pj, pj_hi, pj_lo = sem("pj"), sem("pj_hi"), sem("pj_lo")
        c_T, c_hi, c_lo = sem("c_T"), sem("c_hi"), sem("c_lo")
        v_hi, v_lo = sem("v_hi"), sem("v_lo")
        vn_mm, vn_hi, vn_lo = sem("vn_mm"), sem("vn_hi"), sem("vn_lo")
        scores, negmax, expd, sum_inv = sem("scores"), sem("negmax"), sem("expd"), sem("sum_inv")
        a_T, a_hi, a_lo = sem("a_T"), sem("a_hi"), sem("a_lo")
        attn, attn_out = sem("attn"), sem("attn_out")
        o_T, o_hi, o_lo = sem("o_T"), sem("o_hi"), sem("o_lo")
        wo_mm, x2_ok = sem("wo_mm"), sem("x2_ok")
        x2_stat, x2_rstd, x2_norm, x2_copy = sem("x2_stat"), sem("x2_rstd"), sem("x2_norm"), sem("x2_copy")
        x2_T, x2_Tok = sem("x2_T"), sem("x2_Tok")
        logits, masked, prefix, rows_ok = sem("logits"), sem("masked"), sem("prefix"), sem("rows_ok")
        gap_ready, gap_exp = sem("gap_ready"), sem("gap_exp")
        total, most_ok = sem("total"), sem("most_ok")
        vchain = sem("vchain")
        pchain = sem("pchain")

        ZR = 2
        ZN = RROWS // (128 * ZR)
        ZF = (ROWS - RROWS) // (128 * ZR)

        block = stack.enter_context(nc.Block())

        def hl_matmul(o, lh, ll, rh, rl, n, start=True, stop=True, within=None):
            last = None
            for k in range(n):
                if within is not None and k == n // 2:
                    within()
                first = start and k == 0
                end = stop and k == n - 1
                nc.tensor.matmul(o, lh(k), rh(k), start=first, stop=False)
                nc.tensor.matmul(o, lh(k), rl(k), start=False, stop=False)
                last = nc.tensor.matmul(o, ll(k), rh(k), start=False, stop=end)
            return last

        def transposes(bank, blocks, rows=None):
            last = None
            for col, src, p, f in blocks:
                last = nc.tensor.transpose(bank[0:f, col:col + p], src, ident[0:p, 0:p])
            return last

        W0 = [T[0], T[1], T[2], SC[0]]

        def pe_w_rows(n, k, bank, rs):
            return transposes(bank, [(128 * r, wnat[n % 2][:, r, 128 * k:128 * k + 128], 128, 128) for r in rs])

        def pe_w(pe, n, k, bank):
            if k == 0:
                pe.wait_ge(w_in[n], 16)
            pe_w_rows(n, k, bank, range(KT)).then_inc(w_T, 1)

        def pe_xT(pe, g, a, bank):
            pe.wait_ge(x_norm, g + 1)
            transposes(bank, [(S * k, xn[a][:, 128 * k:128 * k + 128], S, 128)
                              for k in range(KT)]).then_inc(x_T, 1)

        def pe_proj(pe, p, c, bank):
            w = c // 2
            for h in range(2):
                m = 2 * (c % 2) + h
                last = hl_matmul(bank[:, h * 2 * S:(h + 1) * 2 * S],
                                 lambda k: wTh[w][:, k, 128 * m:128 * m + 128],
                                 lambda k: wTl[w][:, k, 128 * m:128 * m + 128],
                                 lambda k: xTh[:, k, :], lambda k: xTl[:, k, :], KT)
            last.then_inc(pj, 1)

        def pe_cT(pe, g, a, k, bank):
            blocks = []
            col = 0
            for j, n in enumerate(CROWS):
                blocks.append((col, cn[a][0:n, j, 128 * k:128 * k + 128], n, 128))
                col += n
            transposes(bank, blocks).then_inc(c_T, 1)

        def pe_vnew(pe, a, bank):
            hl_matmul(bank[0:S, :], lambda k: xTh[:, k, a * S:a * S + S], lambda k: xTl[:, k, a * S:a * S + S],
                      lambda k: wTh[2][:, k, :], lambda k: wTl[2][:, k, :], KT).then_inc(vn_mm, 1)

        def pe_scores(pe, a):
            hl_matmul(SC[a][0:S, 0:KP], lambda k: qTh[:, k, a * S:a * S + S], lambda k: qTl[:, k, a * S:a * S + S],
                      lambda k: kTh[:, k, a, :], lambda k: kTl[:, k, a, :], KT).then_inc(scores, 1)

        def pe_aT(pe, g, a, bank):
            pe.wait_ge(expd, g + 1)
            transposes(bank, [(S * j, ex[a][:, c:c + 128], S, 128)
                              for j, c in enumerate((0, S, S + 128, S + 256))]).then_inc(a_T, 1)

        def pe_attn(pe, g, a, bank, within=None):
            pe.wait_ge(a_lo, g + 1)
            pe.wait_ge(vn_lo, g + 1)
            o = bank[0:S, :]
            nc.tensor.matmul(o, aTh[a][0:S, 0, :], vnh[a][:, :], start=True, stop=False)
            nc.tensor.matmul(o, aTh[a][0:S, 0, :], vnl[a][:, :], start=False, stop=False)
            nc.tensor.matmul(o, aTl[a][0:S, 0, :], vnh[a][:, :], start=False, stop=False)
            for j, n in enumerate(CROWS):
                pe.wait_ge(v_lo, 3 * g + j + 1)
                if j == 2 and within is not None:
                    within()
                nc.tensor.matmul(o, aTh[a][0:n, j + 1, :], vh[a][0:n, j, :], start=False, stop=False)
                nc.tensor.matmul(o, aTh[a][0:n, j + 1, :], vl[a][0:n, j, :], start=False, stop=False)
                last = nc.tensor.matmul(o, aTl[a][0:n, j + 1, :], vh[a][0:n, j, :], start=False, stop=j == 2)
            last.then_inc(attn, 1)

        def pe_oT(pe, g, bank):
            pe.wait_ge(attn_out, g + 1)
            transposes(bank, [(S * k, on[:, 128 * k:128 * k + 128], S, 128)
                              for k in range(KT)]).then_inc(o_T, 1)

        def pe_wo(pe, g, a, bank, within=None):
            pe.wait_ge(o_lo, g + 1)
            hl_matmul(bank[0:S, :], lambda k: oTh[a][:, k, :], lambda k: oTl[a][:, k, :],
                      lambda k: wTh[3][:, k, :], lambda k: wTl[3][:, k, :], KT, within=within).then_inc(wo_mm, 1)

        def pe_x2T(pe, g, a, bank):
            pe.wait_ge(x2_norm, g + 1)
            transposes(bank, [(S * k, xr[a][:, 0, 128 * k:128 * k + 128], S, 128)
                              for k in range(KT)]).then_inc(x2_T, 1)

        def pe_logits(pe, g, a, bank=R):
            pe.wait_ge(x2_Tok, g + 1)
            for k in range(KT):
                last = nc.tensor.matmul(bank[0:S, 8 * a:8 * a + 8], x2T[:, k, :], gwT[:, k, :],
                                        start=k == 0, stop=k == KT - 1)
            last.then_inc(logits, 1)

        def pe_prefix(pe, g, a):
            pe.wait_ge(masked, g + 1)
            o = R[0:S, 16 + 8 * a:24 + 8 * a]
            nc.tensor.matmul(o, tri[:, :], mboth[:, a, :], start=True, stop=False)
            nc.tensor.matmul(o, ones[:, :], msum[:, 1 - a, :], start=False, stop=True).then_inc(prefix, 1)

        m_in = [sem(f"m_in{n}") for n in range(NG)]
        d_in = [sem(f"d_in{n}") for n in range(2)]
        xe_in = [sem(f"xe_in{n}") for n in range(2)]
        mg_T, mg_hi, mg_lo = sem("mg_T"), sem("mg_hi"), sem("mg_lo")
        md_T, md_hi, md_lo = sem("md_T"), sem("md_hi"), sem("md_lo")
        e_T, e_hi, e_lo = sem("e_T"), sem("e_hi"), sem("e_lo")
        gu_mm, silu_ok, h_ok = sem("gu_mm"), sem("silu_ok"), sem("h_ok")
        y_mm, y_ok, yidx_ok = sem("y_mm"), sem("y_ok"), sem("yidx_ok")
        y_added, y_free = sem("y_added"), sem("y_free")
        o_zero, o_scat = sem("o_zero"), sem("o_scat")
        UB = 2 * IT

        LG, LD = GU - 1, DU - 1

        def pe_mT(pe, it, u):
            n = u % NG
            pe.wait_ge(m_in[n], 16 * (it * (UB // NG) + u // NG + 1))
            for w in range(2):
                if u:
                    pe.wait_ge(mg_lo, 2 * (it * UB + u) - 1 + w)
                transposes(T[w], [(128 * k, ng[n][:, w, 128 * k:128 * k + 128], 128, 128)
                                  for k in range(KT)]).then_inc(mg_T, 1)

        def pe_dT(pe, it, u):
            e = u // IT
            i = u % IT
            if i == 0:
                pe.wait_ge(d_in[e % 2], 16 * (it + e // 2 + 1))
            if u:
                pe.wait_ge(md_lo, it * UB + u)
            transposes(T[2], [(128 * r, dn[e % 2][:, r, 128 * i:128 * i + 128], 128, 128)
                              for r in range(KT)]).then_inc(md_T, 1)

        def pe_ahead(pe, it):
            for u in range(LG):
                pe_mT(pe, it, u)
                if u < LD:
                    pe_dT(pe, it, u)

        def pe_eT(e, t, bank):
            transposes(bank, [(128 * k, xe[e][:, t, 128 * k:128 * k + 128], 128, 128)
                              for k in range(KT)]).then_inc(e_T, 1)

        def pe_gu(pe, it, u):
            e = u // IT
            pe.wait_ge(mg_lo, 2 * (it * UB + u) + 2)
            if u % IT == 0:
                pe.wait_ge(e_lo, 2 * (2 * it + e) + 2)
            for w in range(2):
                last = hl_matmul(PJ[u % 2][:, w * CAP:(w + 1) * CAP],
                                 lambda k: wgu[u % GU][w][0][:, 128 * k:128 * k + 128],
                                 lambda k: wgu[u % GU][w][1][:, 128 * k:128 * k + 128],
                                 lambda k: eh[e][:, k, :], lambda k: el_[e][:, k, :], KT)
            last.then_inc(gu_mm, 1)

        def pe_down(pe, it, u):
            i = u % IT
            pe.wait_ge(h_ok, it * UB + u + 1)
            pe.wait_ge(md_lo, it * UB + u + 1)
            if u == IT:
                pe.wait_ge(y_ok, 4 * it + 2)
            b = u % 2
            wh, wl = wdn[u % DU]
            for t in range(2):
                o = SC[t][:, :]
                s = slice(128 * t, 128 * t + 128)
                nc.tensor.matmul(o, hh[b][:, s], wh[:, :], start=i == 0, stop=False)
                nc.tensor.matmul(o, hh[b][:, s], wl[:, :], start=False, stop=False)
                last = nc.tensor.matmul(o, hl[b][:, s], wh[:, :], start=False, stop=i == IT - 1)
            last.then_inc(y_mm, 1)

        def pe_experts(pe, it, more=True):
            for u in range(UB):
                e, i = u // IT, u % IT
                if more or u + LG < UB:
                    pe_mT(pe, it, u + LG)
                if (i == 3 or i == 6) and (more or e == 0):
                    t = i // 6
                    nxt = 2 * it + e + 1
                    if t == 0:
                        pe.wait_ge(xe_in[(e + 1) % 2], 16 * (it + e + 1))
                    pe.wait_ge(e_lo, 2 * nxt + t)
                    pe_eT((e + 1) % 2, t, R)
                pe_gu(pe, it, u)
                if u:
                    pe_down(pe, it, u - 1)
                if more or u + LD < UB:
                    pe_dT(pe, it, u + LD)
            pe_down(pe, it, UB - 1)

        @block.tensor
        def _(pe):
            pe.wait_ge(const_ready, 1)
            pe.wait_ge(wq_half, 16)
            for k in range(KT):
                pe_w_rows(0, k, W0[k], (0, 1))
            pe.wait_ge(w_in[0], 16)
            for k in range(KT):
                pe_w_rows(0, k, W0[k], (2, 3)).then_inc(w_T, 1)
            pe_xT(pe, 0, 0, SC[1])
            pe_xT(pe, 1, 1, R)
            pe.wait_ge(w_lo, 4)
            pe.wait_ge(x_lo, 2)
            pe_proj(pe, 0, 0, PJ[0])
            for k in range(KT):
                pe_w(pe, 1, k, W0[k])
            pe_proj(pe, 0, 1, PJ[1])
            pe.wait_ge(w_lo, 5)
            pe_w(pe, 2, 0, W0[0])
            pe.wait_ge(w_lo, 6)
            pe_w(pe, 2, 1, W0[1])
            pe.wait_ge(w_lo, 8)
            pe.wait_ge(pj_lo, 1)
            pe_proj(pe, 0, 2, PJ[0])
            pe_w(pe, 2, 2, W0[2])
            pe_w(pe, 2, 3, W0[3])
            pe.wait_ge(pj_lo, 2)
            pe_proj(pe, 0, 3, PJ[1])
            pe.wait_ge(gw_in, 16)
            transposes(R, [(8 * k, gwn[:, 128 * k:128 * k + 128], NE, 128) for k in range(KT)]).then_inc(gw_T, 1)
            pe.wait_ge(ctx_in[0], 32)
            pe.wait_ge(w_lo, 9)
            pe_cT(pe, 0, 0, 0, T[0])
            pe_w(pe, 3, 0, SC[1])
            pe.wait_ge(w_lo, 10)
            pe_cT(pe, 0, 0, 1, T[1])
            pe.wait_ge(w_lo, 11)
            pe_cT(pe, 0, 0, 2, T[2])
            pe.wait_ge(c_lo, 1)
            pe_cT(pe, 0, 0, 3, T[0])
            pe.wait_ge(w_lo, 12)
            pe.wait_ge(gw_ok, 1)
            pe_w(pe, 3, 1, R)
            pe.wait_ge(pj_lo, 3)
            pe_vnew(pe, 0, PJ[0])
            pe.wait_ge(w_lo, 13)
            pe_w(pe, 3, 2, SC[1])
            pe.wait_ge(ctx_in[1], 32)
            pe.wait_ge(c_lo, 2)
            pe_cT(pe, 1, 1, 0, T[1])
            pe.wait_ge(c_lo, 3)
            pe_cT(pe, 1, 1, 1, T[2])
            pe.wait_ge(w_lo, 14)
            pe_w(pe, 3, 3, R)
            pe.wait_ge(pj_lo, 4)
            pe.wait_ge(c_lo, 4)
            pe_scores(pe, 0)
            pe_cT(pe, 1, 1, 2, T[0])
            pe.wait_ge(w_lo, 16)
            pe.wait_ge(c_lo, 5)
            pe_cT(pe, 1, 1, 3, T[1])

            def body(p, more):
                A, B, NA = 2 * p, 2 * p + 1, 2 * p + 2
                pe_vnew(pe, 1, PJ[1])
                pe.wait_ge(c_lo, 4 * B + 3)
                pe_aT(pe, A, 0, T[0])
                pe.wait_ge(c_lo, 4 * B + 4)
                pe_scores(pe, 1)
                pe_attn(pe, A, 0, PJ[0], lambda: pe_aT(pe, B, 1, T[1]))
                if more:
                    pe_xT(pe, NA, 0, T[2])
                    pe_xT(pe, NA + 1, 1, T[0])
                pe_oT(pe, A, SC[0])
                pe_attn(pe, B, 1, PJ[1])
                pe_wo(pe, A, 0, PJ[0], lambda: pe_oT(pe, B, SC[1]))
                if more:
                    pe.wait_ge(x_lo, NA + 2)
                    pe_proj(pe, p + 1, 0, PJ[1])
                    pe.wait_ge(x2_ok, A + 1)
                pe_wo(pe, B, 1, PJ[0] if more else PJ[1])
                pe_x2T(pe, A, 0, T[1])
                if more:
                    pe.wait_ge(pj_lo, 4 * p + 5)
                    pe_proj(pe, p + 1, 1, PJ[1])
                pe_logits(pe, A, 0)
                pe_x2T(pe, B, 1, T[2])
                if more:
                    pe.wait_ge(x2_ok, B + 1)
                    pe_proj(pe, p + 1, 2, PJ[0])
                pe_prefix(pe, A, 0)
                pe_logits(pe, B, 1, R if more else PJ[0])
                if more:
                    pe.wait_ge(ctx_in[0], 32 * p + 64)
                    pe_cT(pe, NA, 0, 0, T[0])
                    pe_cT(pe, NA, 0, 1, T[1])
                    pe.wait_ge(pj_lo, 4 * p + 6)
                    pe_proj(pe, p + 1, 3, PJ[1])
                    pe_cT(pe, NA, 0, 2, T[2])
                    pe.wait_ge(c_lo, 4 * NA + 1)
                    pe_cT(pe, NA, 0, 3, T[0])
                pe_prefix(pe, B, 1)
                if not more:
                    pe_ahead(pe, 0)
                if more:
                    pe.wait_ge(pj_lo, 4 * p + 7)
                    pe_vnew(pe, 0, PJ[0])
                    pe.wait_ge(ctx_in[1], 32 * p + 64)
                    pe.wait_ge(c_lo, 4 * NA + 2)
                    pe_cT(pe, NA + 1, 1, 0, T[1])
                    pe.wait_ge(c_lo, 4 * NA + 3)
                    pe_cT(pe, NA + 1, 1, 1, T[2])
                    pe.wait_ge(pj_lo, 4 * p + 8)
                    pe.wait_ge(c_lo, 4 * NA + 4)
                    pe_scores(pe, 0)
                    pe_cT(pe, NA + 1, 1, 2, T[0])
                    pe.wait_ge(c_lo, 4 * NA + 5)
                    pe_cT(pe, NA + 1, 1, 3, T[1])

            with pe.Fori(0, PAIRS - 1) as p:
                body(p, True)
            body(PAIRS - 1, False)

            pe.wait_ge(rows_ok, NB)
            nc.tensor.matmul(SC[1][0:S, 0:8], ones[:, :], msum[:, 1, :], start=True, stop=True).then_inc(total, 1)

            pe.wait_ge(xe_in[0], 16)
            pe_eT(0, 0, R)
            pe_eT(0, 1, SC[0])
            pe.wait_ge(most_ok, 1)
            with pe.Fori(0, NE // 2 - 1) as j:
                pe_experts(pe, j)
            pe_experts(pe, NE // 2 - 1, more=False)
            longest = pe.value_load(mosti[0:1, 0:1], min_val=0, max_val=TOK)
            with pe.If(longest > CAP):
                pe_ahead(pe, NE // 2)
                pe.wait_ge(y_ok, 2 * NE)
                pe.wait_ge(xe_in[0], 16 * (NE // 2 + 1))
                pe_eT(0, 0, R)
                pe_eT(0, 1, SC[0])
                with pe.Fori(NE // 2, ROUNDS * NE // 2 - 1) as j:
                    pe_experts(pe, j)
                pe_experts(pe, ROUNDS * NE // 2 - 1, more=False)

        @block.scalar
        def _(act):
            def copy(o, i, s, n=1):
                nc.scalar.activation(o, i, ACT.Copy).then_inc(s, n)

            def hi_w(n, k, bank):
                act.wait_ge(w_T, 4 * n + k + 1)
                copy(wTh[n][:, k, :], bank[:, :], w_hi)

            def hi_x(g, a, bank):
                act.wait_ge(x_T, g + 1)
                copy(xTh[:, :, a * S:a * S + S], bank[:, 0:KT * S].rearrange("p (k t) -> p k t", k=KT), x_hi)

            def hi_pj(n, c, bank):
                act.wait_ge(pj, n)
                v = bank[:, 0:4 * S].rearrange("p (m t) -> p m t", m=2)
                m = 2 * (c % 2)
                if c < 2:
                    copy(qTh[:, m:m + 2, :], v, pj_hi)
                else:
                    copy(kTh[:, m:m + 2, :, 0:S], v.rearrange("p m (a t) -> p m a t", a=2), pj_hi)

            def hi_c(g, a, k):
                act.wait_ge(c_T, 4 * g + k + 1)
                copy(kTh[:, k, a, CTX:KEYS], T[(k + a) % 3][:, 0:C], c_hi)

            def hi_vn(g, a, bank):
                act.wait_ge(vn_mm, g + 1)
                copy(vnh[a][:, :], bank[0:S, :], vn_hi)

            def hi_v(a, uses):
                act.wait_ge(ctx_in[a], 32 * uses)
                for j, n in enumerate(CROWS):
                    copy(vh[a][0:n, j, :], cn[a][0:n, j, :], v_hi)

            def do_exp(g, a):
                act.wait_ge(negmax, g + 1)
                nc.scalar.activation(ex[a][:, 0:KEYS], SC[a][0:S, 0:KEYS], ACT.Exp, bias=nm[:, a, :],
                                     scale=SCALE, accum_out=esum[:, a, :]).then_inc(expd, 1)

            def hi_a(g, a, bank):
                act.wait_ge(a_T, g + 1)
                copy(aTh[a][:, :, :], bank[:, 0:4 * S].rearrange("p (k t) -> p k t", k=4), a_hi)

            def do_o(g, a, bank):
                act.wait_ge(attn, g + 1)
                act.wait_ge(sum_inv, g + 1)
                nc.scalar.activation(on[:, :], bank[0:S, :], ACT.Copy, scale=rinv[:, a, :]).then_inc(attn_out, 1)

            def hi_o(g, a, bank):
                act.wait_ge(o_T, g + 1)
                copy(oTh[a][:, :, :], bank[:, 0:4 * S].rearrange("p (k t) -> p k t", k=4), o_hi)

            def keep_x2(g, a):
                act.wait_ge(x2_norm, g + 1)
                copy(xr[a][:, 1, 0:D], xr[a][:, 0, 0:D], x2_copy)
                copy(xn2_all[:, g, :], xr[a][:, 0, 0:D], x2_copy)

            def x2T_out(g, bank):
                act.wait_ge(x2_T, g + 1)
                copy(x2T[:, :, :], bank[:, 0:4 * S].rearrange("p (k t) -> p k t", k=4), x2_Tok)

            def gap(g, a):
                act.wait_ge(gap_ready, g + 1)
                nc.scalar.activation(el[:, a, :], dl[:, a, :], ACT.Exp).then_inc(gap_exp, 1)

            for k in range(KT):
                hi_w(0, k, W0[k])
            hi_x(0, 0, SC[1])
            hi_x(1, 1, R)
            hi_pj(1, 0, PJ[0])
            for k in range(KT):
                hi_w(1, k, W0[k])
            hi_pj(2, 1, PJ[1])
            hi_w(2, 0, W0[0])
            hi_w(2, 1, W0[1])
            hi_pj(3, 2, PJ[0])
            hi_w(2, 2, W0[2])
            hi_w(2, 3, W0[3])
            hi_pj(4, 3, PJ[1])
            hi_c(0, 0, 0)
            hi_w(3, 0, SC[1])
            for k in range(1, KT):
                hi_c(0, 0, k)
            hi_w(3, 1, R)
            hi_v(0, 1)
            hi_vn(0, 0, PJ[0])
            hi_w(3, 2, SC[1])
            hi_c(1, 1, 0)
            hi_c(1, 1, 1)
            hi_w(3, 3, R)
            hi_v(1, 1)
            hi_c(1, 1, 2)
            hi_c(1, 1, 3)

            def body(p, more):
                A, B, NA = 2 * p, 2 * p + 1, 2 * p + 2
                do_exp(A, 0)
                hi_vn(B, 1, PJ[1])
                hi_a(A, 0, T[0])
                do_exp(B, 1)
                hi_a(B, 1, T[1])
                do_o(A, 0, PJ[0])
                if more:
                    hi_x(NA, 0, T[2])
                    hi_x(NA + 1, 1, T[0])
                hi_o(A, 0, SC[0])
                do_o(B, 1, PJ[1])
                hi_o(B, 1, SC[1])
                if more:
                    hi_pj(4 * p + 5, 0, PJ[1])
                    keep_x2(A, 0)
                x2T_out(A, T[1])
                if more:
                    hi_pj(4 * p + 6, 1, PJ[1])
                else:
                    keep_x2(A, 0)
                x2T_out(B, T[2])
                keep_x2(B, 1)
                gap(A, 0)
                if more:
                    hi_pj(4 * p + 7, 2, PJ[0])
                    hi_c(NA, 0, 0)
                    hi_c(NA, 0, 1)
                    hi_pj(4 * p + 8, 3, PJ[1])
                    hi_c(NA, 0, 2)
                    hi_c(NA, 0, 3)
                gap(B, 1)
                if not more:
                    hi_ahead(0)
                if more:
                    hi_v(0, p + 2)
                    hi_vn(NA, 0, PJ[0])
                    hi_c(NA + 1, 1, 0)
                    hi_c(NA + 1, 1, 1)
                    hi_v(1, p + 2)
                    hi_c(NA + 1, 1, 2)
                    hi_c(NA + 1, 1, 3)

            def hi_m(it, u):
                for w in range(2):
                    act.wait_ge(mg_T, 2 * (it * UB + u) + 1 + w)
                    copy(wgu[u % GU][w][0][:, :], T[w][:, :], mg_hi)

            def hi_d(it, u):
                act.wait_ge(md_T, it * UB + u + 1)
                copy(wdn[u % DU][0][:, :], T[2][:, :], md_hi)

            def hi_ahead(it):
                for u in range(LG):
                    hi_m(it, u)
                    if u < LD:
                        hi_d(it, u)

            def hi_e(n, e, t, bank):
                act.wait_ge(e_T, n)
                copy(eh[e][:, :, 128 * t:128 * t + 128], bank[:, :].rearrange("p (k s) -> p k s", k=KT), e_hi)

            def y_out(it, e):
                act.wait_ge(y_mm, it * UB + IT * (e + 1))
                act.wait_ge(y_free, 2 * it + e + 1)
                for t in range(2):
                    nc.scalar.activation(ys[:, t, :], SC[t][:, :], ACT.Copy,
                                         scale=xe[e][:, t, D:D + 1]).then_inc(y_ok, 1)

            def experts(it, more=True):
                for u in range(UB):
                    e, i = u // IT, u % IT
                    if more or u + LG < UB:
                        hi_m(it, u + LG)
                    if (i == 3 or i == 6) and (more or e == 0):
                        hi_e(2 * (2 * it + e + 1) + 1 + i // 6, (e + 1) % 2, i // 6, R)
                    act.wait_ge(gu_mm, it * UB + u + 1)
                    nc.scalar.activation(hs[u % 2][:, :], PJ[u % 2][:, 0:CAP], ACT.Silu).then_inc(silu_ok, 1)
                    if i == 0 and e == 1:
                        y_out(it, 0)
                    if more or u + LD < UB:
                        hi_d(it, u + LD)
                y_out(it, 1)

            with act.Fori(0, PAIRS - 1) as p:
                body(p, True)
            body(PAIRS - 1, False)
            hi_e(1, 0, 0, R)
            hi_e(2, 0, 1, SC[0])
            with act.Fori(0, NE // 2 - 1) as j:
                experts(j)
            experts(NE // 2 - 1, more=False)
            act.wait_ge(most_ok, 1)
            longest = act.value_load(mosti[0:1, 0:1], min_val=0, max_val=TOK)
            with act.If(longest > CAP):
                hi_ahead(NE // 2)
                hi_e(2 * NE + 1, 0, 0, R)
                hi_e(2 * NE + 2, 0, 1, SC[0])
                with act.Fori(NE // 2, ROUNDS * NE // 2 - 1) as j:
                    experts(j)
                experts(ROUNDS * NE // 2 - 1, more=False)

        @block.vector
        def _(dve):
            v = nc.vector
            def lo(o, psum, hi, s):
                v.tensor_tensor(o, psum, hi.bitcast(F32), ALU.subtract).then_inc(s, 1)

            chain = [0, 0]

            def link(ins, plain=False):
                ins.then_inc(vchain, 1)
                chain[1] += 1
                dve.wait_ge(vchain, chain[0] + chain[1])
                if plain:
                    met()

            def met():
                v.memset(spare[0:1, 0:1], 0.0)

            def lo_w(n, k, bank):
                dve.wait_ge(w_hi, 4 * n + k + 1)
                lo(wTl[n][:, k, :], bank[:, :], wTh[n][:, k, :], w_lo)

            def stat_x(g, n, part):
                for b in range(g, g + n):
                    link(v.bn_stats(st[:, b % 2, :], x_all[:, b, :]), plain=True)
                    link(v.bn_aggr(mr_all[:, b, :], st[:, b % 2, :]))
                if part:
                    v.tensor_scalar(ve_all[:, part[0]:part[1]], mr_all[:, part[0]:part[1], 1], EPS, None, ALU.add)\
                        .then_inc(x_stat, 1)

            def norm_x(g, powers):
                dve.wait_ge(x_rstd, powers)
                link(v.tensor_copy(mr[:, :, :], mr_all[:, bass.ds(g, 2), :]))
                for a in range(2):
                    v.tensor_scalar(xn[a][:, :], x_all[:, g + a, :], mr[:, a, 0:1], mr[:, a, 1:2],
                                    ALU.subtract, ALU.mult).then_inc(x_norm, 1)

            def lo_x(g, a, bank):
                dve.wait_ge(x_hi, g + 1)
                lo(xTl[:, :, a * S:a * S + S], bank[:, 0:KT * S].rearrange("p (k t) -> p k t", k=KT),
                   xTh[:, :, a * S:a * S + S], x_lo)

            def lo_pj(n, c, bank):
                dve.wait_ge(pj_hi, n)
                w = bank[:, 0:4 * S].rearrange("p (m t) -> p m t", m=2)
                m = 2 * (c % 2)
                if c < 2:
                    lo(qTl[:, m:m + 2, :], w, qTh[:, m:m + 2, :], pj_lo)
                else:
                    lo(kTl[:, m:m + 2, :, 0:S], w.rearrange("p m (a t) -> p m a t", a=2),
                       kTh[:, m:m + 2, :, 0:S], pj_lo)

            def lo_c(g, a, k):
                dve.wait_ge(c_hi, 4 * g + k + 1)
                lo(kTl[:, k, a, CTX:KEYS], T[(k + a) % 3][:, 0:C], kTh[:, k, a, CTX:KEYS], c_lo)

            def lo_vn(g, a, bank):
                dve.wait_ge(vn_hi, g + 1)
                lo(vnl[a][:, :], bank[0:S, :], vnh[a][:, :], vn_lo)

            def do_max(g, a):
                dve.wait_ge(scores, g + 1)
                link(v.reduce_max(mx[:, a, :], SC[a][0:S, 0:KEYS], AX.X))
                v.tensor_scalar(nm[:, a, :], mx[:, a, :], -SCALE, None, ALU.mult).then_inc(negmax, 1)

            def inv(g, a):
                dve.wait_ge(expd, g + 1)
                v.reciprocal(rinv[:, a, :], esum[:, a, :]).then_inc(sum_inv, 1)

            def lo_a(g, a, bank):
                dve.wait_ge(a_hi, g + 1)
                lo(aTl[a][:, :, :], bank[:, 0:4 * S].rearrange("p (k t) -> p k t", k=4), aTh[a][:, :, :], a_lo)

            def lo_o(g, a, bank):
                dve.wait_ge(o_hi, g + 1)
                lo(oTl[a][:, :, :], bank[:, 0:4 * S].rearrange("p (k t) -> p k t", k=4), oTh[a][:, :, :], o_lo)

            def x2_stats(g, a, bank):
                dve.wait_ge(wo_mm, g + 1)
                v.tensor_tensor(x_all[:, g, :], bank[0:S, :], x_all[:, g, :], ALU.add).then_inc(x2_ok, 1)
                dve.wait_ge(x2_ok, g + 1)
                met()
                link(v.bn_stats(st2[:, a, :], x_all[:, g, :]), plain=True)
                link(v.bn_aggr(mv2[:, a, :], st2[:, a, :]))
                v.tensor_scalar(ve2[:, a, :], mv2[:, a, 1:2], EPS, None, ALU.add).then_inc(x2_stat, 1)

            def x2_norms(g, a, used):
                dve.wait_ge(x2_rstd, g + 1)
                dve.wait_ge(row_free[a], used)
                v.tensor_scalar(xr[a][:, 0, 0:D], x_all[:, g, :], mv2[:, a, 0:1], rs2[:, a, :],
                                ALU.subtract, ALU.mult).then_inc(x2_norm, 1)

            def topk(g, a, bank=R):
                dve.wait_ge(logits, g + 1)
                if a and bank is R:
                    dve.wait_ge(prefix, g)
                    v.tensor_copy(pos[:, 0, :], R[0:S, 16:24])
                link(v.tensor_copy(lgs[:, a, :], bank[0:S, 8 * a:8 * a + 8]), plain=True)
                link(v.max(mx8[:, a, :], lgs[:, a, :]), plain=True)
                link(v.max_index(ix8[:, a, :], mx8[:, a, :], lgs[:, a, :]))
                link(v.tensor_copy(ixf[:, a, :], ix8[:, a, 0:2]))
                v.tensor_scalar(mask[:, a, 0, :], iota8[:, :], ixf[:, a, 0:1], None, ALU.is_equal)
                link(v.tensor_scalar(mask[:, a, 1, :], iota8[:, :], ixf[:, a, 1:2], None, ALU.is_equal))
                v.tensor_tensor(mboth[:, a, :], mask[:, a, 0, :], mask[:, a, 1, :], ALU.add).then_inc(masked, 1)
                v.tensor_tensor(dl[:, a, :], mx8[:, a, 1:2], mx8[:, a, 0:1], ALU.subtract).then_inc(gap_ready, 1)
                dve.wait_ge(masked, g + 1)
                link(v.tensor_tensor(msum[:, a, :], msum[:, 1 - a, :], mboth[:, a, :], ALU.add))

            def read_pos():
                dve.wait_ge(prefix, NB - 1)
                link(v.tensor_copy(pos[:, 0, :], R[0:S, 16:24]))

            def weights(g, a):
                dve.wait_ge(gap_exp, g + 1)
                link(v.tensor_scalar(el1[:, a, :], el[:, a, :], 1.0, None, ALU.add))
                link(v.reciprocal(wts[:, a, 0:1], el1[:, a, :]))
                link(v.tensor_tensor(wts[:, a, 1:2], el[:, a, :], wts[:, a, 0:1], ALU.mult))
                v.tensor_copy(w_all[:, g, :], wts[:, a, :])
                v.tensor_copy(xr[a][:, :, D], wts[:, a, :])
                v.tensor_scalar(xr[a][:, :, D + 1], xr[a][:, :, D + 1], 2.0 * S, None, ALU.add)

            def rows(g, a):
                if a:
                    dve.wait_ge(prefix, g + 1)
                    link(v.tensor_copy(pos[:, 1, :], R[0:S, 24:32]))
                v.tensor_tensor(rb[:, a, :], pos[:, a, :], ebase[:, :], ALU.add)
                link(v.tensor_scalar(rr[:, a, :], pos[:, a, :], float(CAP), None, ALU.is_ge))
                link(v.scalar_tensor_tensor(rr2[:, a, :], pos[:, a, :], 2.0 * CAP, rr[:, a, :], ALU.is_ge, ALU.add))
                link(v.scalar_tensor_tensor(rr3[:, a, :], pos[:, a, :], 3.0 * CAP, rr2[:, a, :], ALU.is_ge, ALU.add))
                link(v.scalar_tensor_tensor(row8[:, a, :], rr3[:, a, :], float(RROWS - CAP), rb[:, a, :],
                                            ALU.mult, ALU.add))
                v.tensor_tensor(junk[:, a, 0, :], row8[:, a, :], mask[:, a, 0, :], ALU.mult)
                link(v.tensor_tensor(junk[:, a, 1, :], row8[:, a, :], mask[:, a, 1, :], ALU.mult))
                link(v.reduce_sum(rowf[:, a, :], junk[:, a, :, :], AX.X))
                v.tensor_copy(idx[a][0][:, :], rowf[:, a, 0:1])
                v.tensor_copy(idx[a][1][:, :], rowf[:, a, 1:2])
                v.tensor_copy(row_all[:, g, :], rowf[:, a, :]).then_inc(rows_ok, 1)

            dve.wait_ge(const_ready, 3)
            dve.wait_ge(x_in[0], 16)
            stat_x(0, 2, (0, 2))
            norm_x(0, 1)
            for k in range(KT):
                lo_w(0, k, W0[k])
            lo_x(0, 0, SC[1])
            lo_x(1, 1, R)
            lo_pj(1, 0, PJ[0])
            for k in range(KT):
                lo_w(1, k, W0[k])
            lo_pj(2, 1, PJ[1])
            lo_w(2, 0, W0[0])
            lo_w(2, 1, W0[1])
            lo_pj(3, 2, PJ[0])
            lo_w(2, 2, W0[2])
            lo_w(2, 3, W0[3])
            dve.wait_ge(x_in[1], 16)
            stat_x(2, 1, None)
            lo_pj(4, 3, PJ[1])
            stat_x(3, 1, None)
            dve.wait_ge(gw_T, 1)
            v.tensor_copy(gwT[:, :, :], R[:, 0:KT * NE].rearrange("p (k e) -> p k e", k=KT)).then_inc(gw_ok, 1)
            lo_c(0, 0, 0)
            lo_w(3, 0, SC[1])
            for k in range(1, KT):
                lo_c(0, 0, k)
            lo_w(3, 1, R)
            stat_x(4, 2, None)
            lo_vn(0, 0, PJ[0])
            lo_w(3, 2, SC[1])
            lo_c(1, 1, 0)
            lo_c(1, 1, 1)
            lo_w(3, 3, R)
            do_max(0, 0)
            lo_c(1, 1, 2)
            lo_c(1, 1, 3)
            stat_x(6, 2, (2, NB))
            def body(p, more):
                A, B, NA = 2 * p, 2 * p + 1, 2 * p + 2
                lo_vn(B, 1, PJ[1])
                inv(A, 0)
                lo_a(A, 0, T[0])
                do_max(B, 1)
                if more:
                    norm_x(NA, 2)
                lo_a(B, 1, T[1])
                inv(B, 1)
                if more:
                    lo_x(NA, 0, T[2])
                    lo_x(NA + 1, 1, T[0])
                lo_o(A, 0, SC[0])
                lo_o(B, 1, SC[1])
                x2_stats(A, 0, PJ[0])
                x2_norms(A, 0, p + 1)
                if more:
                    lo_pj(4 * p + 5, 0, PJ[1])
                x2_stats(B, 1, PJ[0] if more else PJ[1])
                x2_norms(B, 1, p + 1)
                if more:
                    lo_pj(4 * p + 6, 1, PJ[1])
                    topk(A, 0)
                    lo_pj(4 * p + 7, 2, PJ[0])
                    lo_c(NA, 0, 0)
                    lo_c(NA, 0, 1)
                    topk(B, 1)
                    lo_pj(4 * p + 8, 3, PJ[1])
                    lo_c(NA, 0, 2)
                    lo_c(NA, 0, 3)
                    weights(A, 0)
                    rows(A, 0)
                    lo_vn(NA, 0, PJ[0])
                    lo_c(NA + 1, 1, 0)
                    lo_c(NA + 1, 1, 1)
                    weights(B, 1)
                    do_max(NA, 0)
                    lo_c(NA + 1, 1, 2)
                    lo_c(NA + 1, 1, 3)
                    rows(B, 1)
                else:
                    topk(A, 0)
                    weights(A, 0)
                    read_pos()
                    rows(A, 0)
                    topk(B, 1, PJ[0])
                    weights(B, 1)
                    rows(B, 1)
                    lo_ahead(0)

            def lo_m(it, u):
                for w in range(2):
                    dve.wait_ge(mg_hi, 2 * (it * UB + u) + 1 + w)
                    lo(wgu[u % GU][w][1][:, :], T[w][:, :], wgu[u % GU][w][0][:, :], mg_lo)

            def lo_d(it, u):
                dve.wait_ge(md_hi, it * UB + u + 1)
                lo(wdn[u % DU][1][:, :], T[2][:, :], wdn[u % DU][0][:, :], md_lo)

            def lo_ahead(it):
                for u in range(LG):
                    lo_m(it, u)
                    if u < LD:
                        lo_d(it, u)

            def lo_e(n, e, t, bank):
                dve.wait_ge(e_hi, n)
                lo(el_[e][:, :, 128 * t:128 * t + 128], bank[:, :].rearrange("p (k s) -> p k s", k=KT),
                   eh[e][:, :, 128 * t:128 * t + 128], e_lo)

            def experts(it, more=True):
                for u in range(UB):
                    e, i = u // IT, u % IT
                    b = u % 2
                    if more or u + LG < UB:
                        lo_m(it, u + LG)
                    if (i == 3 or i == 6) and (more or e == 0):
                        lo_e(2 * (2 * it + e + 1) + 1 + i // 6, (e + 1) % 2, i // 6, R)
                    if i == 4:
                        link(v.scalar_tensor_tensor(yidt[:, e, :], xe[e][:, :, D + 1], 0.0, padid[:, :],
                                                    ALU.is_equal, ALU.mult))
                        v.scalar_tensor_tensor(yidx[:, e, :], xe[e][:, :, D + 1], -1.0, yidt[:, e, :],
                                               ALU.add, ALU.add).then_inc(yidx_ok, 1)
                    dve.wait_ge(silu_ok, it * UB + u + 1)
                    link(v.tensor_tensor(hf[b][:, :], PJ[b][:, CAP:2 * CAP], hs[b][:, :], ALU.mult))
                    link(v.tensor_copy(hh[b][:, :], hf[b][:, :]))
                    v.tensor_tensor(hl[b][:, :], hf[b][:, :], hh[b][:, :].bitcast(F32), ALU.subtract)\
                        .then_inc(h_ok, 1)
                    if more or u + LD < UB:
                        lo_d(it, u + LD)

            def looped(first, last, f):
                before = chain[0] + chain[1]
                per = LINKS[f.__name__]
                with dve.Fori(first, last) as p:
                    chain[0], chain[1] = before + (p - first) * per, 0
                    f(p, True)
                    assert chain[1] == per, (f.__name__, chain[1])
                chain[0], chain[1] = before + (last - first) * per, 0

            LINKS = {"body": 38, "experts": 34}
            looped(0, PAIRS - 1, body)
            body(PAIRS - 1, False)
            dve.wait_ge(total, 1)
            link(v.reduce_max(most[:, 0:1], SC[1][0:S, 0:8], AX.X))
            v.tensor_copy(mosti[:, 0:1], most[:, 0:1]).then_inc(most_ok, 1)
            lo_e(1, 0, 0, R)
            lo_e(2, 0, 1, SC[0])
            dve.wait_ge(most_ok, 1)
            looped(0, NE // 2 - 1, experts)
            experts(NE // 2 - 1, False)
            longest = dve.value_load(mosti[0:1, 0:1], min_val=0, max_val=TOK)
            with dve.If(longest > CAP):
                lo_ahead(NE // 2)
                lo_e(2 * NE + 1, 0, 0, R)
                lo_e(2 * NE + 2, 0, 1, SC[0])
                looped(NE // 2, ROUNDS * NE // 2 - 1, experts)
                experts(ROUNDS * NE // 2 - 1, False)

        @block.gpsimd
        def _(pool):
            g_ = nc.gpsimd
            g_.memset(ident[:, :], 0.0).then_inc(const_step, 1)
            pool.wait_ge(const_step, 1)
            g_.affine_select(out=ident[:, :], in_=ident[:, :], compare_op=ALU.not_equal, fill=1.0, base=0,
                             pattern=[[-1, 128]], channel_multiplier=1).then_inc(const_ready, 1)
            g_.memset(half[:, :], -0.5).then_inc(const_step, 1)
            g_.memset(zero[:, :], 0.0).then_inc(const_step, 1)
            for a in range(2):
                g_.memset(kTh[:, :, a, KEYS:KP].bitcast(F32), 0.0).then_inc(const_step, 1)
                g_.memset(kTl[:, :, a, KEYS:KP].bitcast(F32), 0.0).then_inc(const_step, 1)
                g_.memset(ex[a][:, KEYS:512], 0.0).then_inc(const_step, 1)
            g_.memset(ones[:, :], 1.0).then_inc(const_step, 1)
            g_.memset(tri[:, :], 1.0).then_inc(const_step, 1)
            g_.memset(msum[:, 1, :], 0.0).then_inc(const_step, 1)
            g_.iota(iotai[0:S, 0:8], pattern=[[1, 8]], base=0, channel_multiplier=0).then_inc(const_step, 1)
            g_.iota(iotai[0:S, 8:16], pattern=[[CAP, 8]], base=0, channel_multiplier=0).then_inc(const_step, 1)
            g_.iota(iotai[:, 16:18], pattern=[[128, 2]], base=TOK + 1, channel_multiplier=1).then_inc(const_step, 1)
            g_.iota(iotai[0:S, 18:20], pattern=[[0, 2]], base=1 - 2 * S, channel_multiplier=1)\
                .then_inc(const_step, 1)
            pool.wait_ge(const_step, 16)
            g_.affine_select(out=tri[:, :], in_=tri[:, :], compare_op=ALU.is_gt, fill=0.0, base=0,
                             pattern=[[1, S]], channel_multiplier=-1).then_inc(const_step, 1)
            g_.tensor_copy(iota8[:, :], iotai[0:S, 0:8]).then_inc(const_step, 1)
            g_.tensor_copy(ebase[:, :], iotai[0:S, 8:16]).then_inc(const_step, 1)
            g_.tensor_copy(padid[:, :], iotai[:, 16:18]).then_inc(const_step, 1)
            g_.tensor_copy(xr[0][:, :, D + 1], iotai[0:S, 18:20]).then_inc(const_step, 1)
            g_.tensor_scalar(xr[1][:, :, D + 1], iotai[0:S, 18:20], float(S), None, ALU.add).then_inc(const_step, 1)
            pool.wait_ge(const_step, 22)
            flag = [0]

            def signal(s, n=1):
                g_.memset(flags[0:1, flag[0]:flag[0] + 1], 0.0).then_inc(s, n)
                flag[0] += 1

            signal(row_free[0])
            signal(row_free[1])
            signal(y_free)
            signal(const_ready, 2)

            def power(o, i, ready, n, done):
                pool.wait_ge(ready, n)
                g_.tensor_tensor(o, i, half[0:S, 0:1], ALU.pow).then_inc(done, 1)

            def lo_v(g, a):
                pool.wait_ge(c_T, 4 * g + 4)
                for j, n in enumerate(CROWS):
                    pool.wait_ge(v_hi, 3 * g + j + 1)
                    g_.tensor_tensor(vl[a][0:n, j, :], cn[a][0:n, j, :], vh[a][0:n, j, :].bitcast(F32),
                                     ALU.subtract).then_inc(v_lo, 1)

            def scatter(g, a):
                pool.wait_ge(rows_ok, g + 1)
                pool.wait_ge(x2_copy, 2 * g + 2)
                for s in range(2):
                    pool.indirect_dma_start(slots[:, :], bass.IndirectOffsetOnAxis(idx[a][s][:, :], 0),
                                            xr[a][:, s, :], None).then_inc(scattered[a], 16)

            def powers(a, b, n):
                pool.wait_ge(x_stat, n)
                g_.tensor_tensor(mr_all[:, a:b, 1], ve_all[:, a:b], half[0:S, 0:b - a], ALU.pow).then_inc(x_rstd, 1)

            powers(0, 2, 1)
            lo_v(0, 0)
            lo_v(1, 1)
            powers(2, NB, 2)
            pool.wait_ge(zeroed, 16 * ZN)

            def body(p, more):
                A, B, NA = 2 * p, 2 * p + 1, 2 * p + 2
                if p:
                    for a in range(2):
                        pool.wait_ge(scattered[a], 32 * p)
                        signal(row_free[a])
                power(rs2[:, 0, :], ve2[:, 0, :], x2_stat, A + 1, x2_rstd)
                power(rs2[:, 1, :], ve2[:, 1, :], x2_stat, B + 1, x2_rstd)
                if more:
                    lo_v(NA, 0)
                scatter(A, 0)
                if more:
                    lo_v(NA + 1, 1)
                scatter(B, 1)

            for p in range(PAIRS):
                body(p, p < PAIRS - 1)

            def add_y(n, e):
                pool.wait_ge(yidx_ok, n + 1)
                for t in range(2):
                    pool.wait_ge(y_ok, 2 * n + 1 + t)
                    pool.indirect_dma_start(out[:, :], bass.IndirectOffsetOnAxis(yidx[:, e, t:t + 1], 0),
                                            ys[:, t, :], None, compute_op=ALU.add).then_inc(y_added, 16)
                pool.wait_ge(y_added, 32 * n + 32)
                signal(y_free)

            pool.wait_ge(x2_out, 16 * NB + 16 * 2)
            for n in range(NE):
                add_y(n, n % 2)
            pool.wait_ge(most_ok, 1)
            longest = pool.value_load(mosti[0:1, 0:1], min_val=0, max_val=TOK)
            with pool.If(longest > CAP):
                pool.wait_ge(o_zero, 16 * ZF)
                for a in range(2):
                    g_.tensor_scalar(xr[0][:, a, D + 1:D + 2], xr[0][:, a, D + 1:D + 2], -float(TOK), None, ALU.add)\
                        .then_inc(pchain, 1)
                for g in range(NB):
                    pool.wait_ge(pchain, 2 + 7 * g)
                    if g:
                        pool.wait_ge(o_scat, 32 * g)
                    for s in range(2):
                        g_.tensor_copy(xr[0][:, s, 0:D], xn2_all[:, g, :]).then_inc(pchain, 1)
                        g_.tensor_copy(idx[0][s][:, :], row_all[:, g, s:s + 1]).then_inc(pchain, 1)
                        g_.tensor_scalar(xr[0][:, s, D + 1:D + 2], xr[0][:, s, D + 1:D + 2], float(2 * S if g == 0 else S),
                                         None, ALU.add).then_inc(pchain, 1)
                    g_.tensor_copy(xr[0][:, :, D], w_all[:, g, :]).then_inc(pchain, 1)
                    pool.wait_ge(pchain, 9 + 7 * g)
                    for s in range(2):
                        pool.indirect_dma_start(slots[:, :], bass.IndirectOffsetOnAxis(idx[0][s][:, :], 0),
                                                xr[0][:, s, :], None).then_inc(o_scat, 16)
                for n in range(NE, ROUNDS * NE):
                    add_y(n, n % 2)

        @block.sync
        def _(sp):
            xv = x.rearrange("b s d -> s b d")
            ws = [wq, wk, wv, wo]

            def load_w(n):
                sp.dma_start(wnat[n % 2][:, :, :], ws[n].rearrange("(r p) d -> p r d", p=128)).then_inc(w_in[n], 16)

            def load_ctx(g, a):
                sp.dma_start(cn[a][:, 0:2, :], ctxt[g, 0:256, :].rearrange("(j p) d -> p j d", p=128))\
                    .then_inc(ctx_in[a], 16)
                sp.dma_start(cn[a][0:CROWS[2], 2, :], ctxt[g, 256:C, :]).then_inc(ctx_in[a], 16)

            wqv = wq.rearrange("(r p) d -> p r d", p=128)
            sp.dma_start(x_all[:, 0:2, :], xv[:, 0:2, :]).then_inc(x_in[0], 16)
            sp.dma_start(wnat[0][:, 0:2, :], wqv[:, 0:2, :]).then_inc(wq_half, 16)
            sp.dma_start(wnat[0][:, 2:KT, :], wqv[:, 2:KT, :]).then_inc(w_in[0], 16)
            load_w(1)
            sp.dma_start(gwn[:, :], gate_w).then_inc(gw_in, 16)
            load_ctx(0, 0)
            sp.wait_ge(w_T, 4)
            load_w(2)
            sp.dma_start(x_all[:, 2:NB, :], xv[:, 2:NB, :]).then_inc(x_in[1], 16)
            load_ctx(1, 1)
            sp.wait_ge(w_T, 8)
            load_w(3)
            sp.wait_ge(const_step, 3)
            for n in range(ZN):
                sp.dma_start(slots[256 * n:256 * n + 256, :].rearrange("(p r) w -> p (r w)", p=128),
                             zero[:, :]).then_inc(zeroed, 16)

            def store_x2(g):
                sp.wait_ge(x2_ok, g + 1)
                sp.dma_start(out[bass.ds(g * S, S), :], x_all[:, g, :]).then_inc(x2_out, 16)

            with sp.Fori(0, PAIRS - 1) as p:
                sp.wait_ge(attn, 2 * p + 1)
                load_ctx(2 * p + 2, 0)
                sp.wait_ge(attn, 2 * p + 2)
                load_ctx(2 * p + 3, 1)
                store_x2(2 * p)
                store_x2(2 * p + 1)

            def load_m(e, i, n):
                sp.dma_start(ng[n][:, :, :],
                             gate_up.rearrange("e (w i p) d -> e i p w d", w=2, p=128)[e, i, :, :, :])\
                    .then_inc(m_in[n], 16)

            def load_d(e, par):
                sp.dma_start(dn[par][:, :, :], down.rearrange("e (r p) i -> e p r i", p=128)[e, :, :, :])\
                    .then_inc(d_in[par], 16)

            sp.wait_ge(pj, 4 * PAIRS)
            load_m(0, 0, 0)
            load_d(0, 0)
            for i in range(1, NG):
                load_m(0, i, i)
            sp.wait_ge(vn_mm, NB)
            load_d(1, 1)
            store_x2(NB - 2)
            store_x2(NB - 1)
            for n in range(2):
                sp.dma_start(out[TOK + 128 * n:TOK + 128 * n + 128, :], zero[:, 0:D]).then_inc(x2_out, 16)

            def load_xe(n, par):
                sp.dma_start(xe[par][:, :, :],
                             slots[bass.ds(n * CAP, CAP), :].rearrange("(t p) w -> p t w", p=128))\
                    .then_inc(xe_in[par], 16)

            def load_ahead(it, us):
                for u in us:
                    sp.wait_ge(mg_T, 2 * (it * UB + u) + 2)
                    load_m((u + NG) // IT, (u + NG) % IT, u % NG)

            load_ahead(0, range(NG - 1))
            sp.wait_ge(x2_out, 16 * NB + 16 * 2)
            for a in range(2):
                sp.wait_ge(scattered[a], 32 * PAIRS)
            load_xe(0, 0)
            load_xe(1, 1)
            load_ahead(0, range(NG - 1, LG))

            def experts(it, e0, e2, more=True):
                for u in range(UB):
                    if u == LG - 2 and more:
                        sp.wait_ge(md_T, it * UB + IT)
                        load_d(e2, 0)
                    if u == IT + 1 and more:
                        sp.wait_ge(y_ok, 4 * it + 2)
                        sp.wait_ge(yidx_ok, 2 * it + 1)
                        load_xe(2 * it + 2, 0)
                    if u == UB - 3 and more:
                        sp.wait_ge(md_T, it * UB + UB)
                        load_d(e2 + 1, 1)
                    uu = u + LG + NG
                    if more or uu < UB:
                        sp.wait_ge(mg_T, 2 * (it * UB + u + LG) + 2)
                        load_m(e0 + uu // IT if uu < UB else e2 + uu // IT - 2, uu % IT, uu % NG)
                if more:
                    sp.wait_ge(y_ok, 4 * it + 4)
                    sp.wait_ge(yidx_ok, 2 * it + 2)
                    load_xe(2 * it + 3, 1)

            with sp.Fori(0, NE // 2 - 1) as j:
                experts(j, 2 * j, 2 * j + 2)
            experts(NE // 2 - 1, NE - 2, 0, more=False)

            sp.wait_ge(most_ok, 1)
            longest = sp.value_load(mosti[0:1, 0:1], min_val=0, max_val=TOK)
            with sp.If(longest > CAP):
                for n in range(ZF):
                    r = RROWS + 128 * ZR * n
                    sp.dma_start(slots[r:r + 128 * ZR, :].rearrange("(p r) w -> p (r w)", p=128), zero[:, :])\
                        .then_inc(o_zero, 16)
                sp.wait_ge(mg_T, 2 * NE * IT)
                sp.wait_ge(md_T, NE * IT)
                for i in range(NG):
                    load_m(0, i, i)
                load_d(0, 0)
                load_d(1, 1)
                load_ahead(NE // 2, range(LG))
                sp.wait_ge(o_scat, 32 * NB)
                sp.wait_ge(y_ok, 2 * NE)
                sp.wait_ge(yidx_ok, NE)
                load_xe(NE, 0)
                load_xe(NE + 1, 1)

                def first_bodies(r):
                    with sp.Fori(0, NE // 2 - 1) as j:
                        experts(r * (NE // 2) + j, 2 * j, 2 * j + 2)

                with sp.Fori(1, ROUNDS - 1) as r:
                    first_bodies(r)
                    experts(r * (NE // 2) + NE // 2 - 1, NE - 2, 0)
                first_bodies(ROUNDS - 1)
                experts(ROUNDS * (NE // 2) - 1, NE - 2, 0, more=False)


_INS = ["x", "ctx_2048", "L0_xattn_wq", "L0_xattn_wk", "L0_xattn_wv", "L0_xattn_wo", "L0_ffn_gate_weight",
        "L0_ffn_gate_up_proj", "L0_ffn_down_proj"]


def kernel(**inputs):
    import numpy as _np
    import concourse.bacc as _bacc
    from concourse import mybir as _mybir
    from concourse.bass_utils import run_bass_kernel_spmd as _run

    nc = _bacc.Bacc("TRN2", target_bir_lowering=False, num_devices=1)
    arrays, args = {}, []
    for name in _INS:
        a = _np.ascontiguousarray(inputs[name])
        arrays[f"in_{name}"] = a
        args.append(nc.dram_tensor(f"in_{name}", a.shape, _mybir.dt.from_np(a.dtype), kind="ExternalInput").ap())
    args.append(nc.dram_tensor("out", (OUTR, D), _mybir.dt.float32, kind="ExternalOutput").ap())
    build_kernel(nc, *args)
    r = _run(nc, [arrays], core_ids=[0])
    return r.results[0]["out"][0:TOK].reshape(NB, S, D)
```
